# Optimizing a Trainium2 kernel written in Bass

```python
import numpy as np
import jax
import jax.numpy as jnp

def _softmax(x, axis=-1):
    return jax.nn.softmax(x, axis=axis)

def _gelu(x):
    return jax.nn.gelu(x, approximate=True)

def _silu(x):
    return jax.nn.silu(x)

def _sigmoid(x):
    return jax.nn.sigmoid(x)

def _layernorm(x, axis=-1, eps=1e-05):
    m = jnp.mean(x, axis=axis, keepdims=True)
    v = jnp.var(x, axis=axis, keepdims=True)
    return (x - m) / jnp.sqrt(v + eps)

def _scatter_add(tgt, idx, src, axis=0):
    return tgt.at[idx].add(src)

def _segment_sum(src, seg, n):
    return jax.ops.segment_sum(src, seg, n)
kernel_name = 'mk_xattn_seq_d2_seqx_r8_e86f39'

def setup_inputs(seed: int=0):
    np.random.seed(seed)
    _w = jnp.asarray

    def _rec_inputs():
        import jax
        import jax.numpy as jnp
        _rk = jax.random.key(seed)
        x = -0.0005207 + 1.001 * jax.random.normal(jax.random.fold_in(_rk, 1), (2, 512, 128), jnp.float32)
        _lenS = 512 - jax.random.randint(jax.random.fold_in(_rk, 7), (2,), 0, max(1, 512 // 4) + 1, jnp.int32)
        _lenS2 = 77 - jax.random.randint(jax.random.fold_in(_rk, 8), (2,), 0, max(1, 77 // 4) + 1, jnp.int32)
        _ctx_1024P = jax.random.normal(jax.random.fold_in(_rk, 11), (2, 16, 128), jnp.float32)
        _ctx_1024c = jax.random.dirichlet(jax.random.fold_in(_rk, 511), 0.3 * jnp.ones((16,), jnp.float32), (2, 77))
        _ctx_1024t = jnp.einsum('bsk,bkd->bsd', _ctx_1024c, _ctx_1024P)
        _ctx_1024t = _ctx_1024t * jax.lax.rsqrt(jnp.mean(jnp.square(_ctx_1024t)) + 1e-12) * 0.953939
        ctx_1024 = 4.13588e-05 + 0.999923 * (_ctx_1024t + 0.3 * jax.random.normal(jax.random.fold_in(_rk, 611), (2, 77, 128), jnp.float32))
        return (x, ctx_1024)
    x, ctx_1024 = _rec_inputs()

    def _L0_xattn_setup():
        import jax, jax.numpy as jnp
        import numpy as np
        D, H, E, K, DFF = (128, 16, 8, 2, 512)
        B, L, T = (4, 64, 256)
        EPS = 1e-05

        def _xavier(key, shape):
            fan_in, fan_out = (shape[-1], shape[-2])
            a = jnp.sqrt(6.0 / (fan_in + fan_out))
            return jax.random.uniform(key, shape, jnp.float32, -a, a)

        def _ln(x, g, b):
            m = x.mean(-1, keepdims=True)
            v = ((x - m) ** 2).mean(-1, keepdims=True)
            return (x - m) / jnp.sqrt(v + EPS) * g + b

        def _mha(q_in, kv_in, in_w, in_b, out_w, out_b):
            wq, wk, wv = jnp.split(in_w, 3, axis=0)
            bq, bk, bv = jnp.split(in_b, 3, axis=0)
            dh = D // H

            def heads(x, w, b):
                y = x @ w.T + b
                return y.reshape(x.shape[0], x.shape[1], H, dh).transpose(0, 2, 1, 3)
            q = heads(q_in, wq, bq)
            k = heads(kv_in, wk, bk)
            v = heads(kv_in, wv, bv)
            scores = jnp.einsum('bhqd,bhkd->bhqk', q, k) / jnp.sqrt(jnp.float32(dh))
            attn = jax.nn.softmax(scores, axis=-1)
            out = jnp.einsum('bhqk,bhkd->bhqd', attn, v)
            out = out.transpose(0, 2, 1, 3).reshape(q_in.shape[0], q_in.shape[1], D)
            return out @ out_w.T + out_b

        def _fuse_moe(x, ln_g, ln_b, rw, rb, fc1_w, fc1_b, fc2_w, fc2_b):
            h = _ln(x, ln_g, ln_b)
            logits = h @ rw.T + rb
            vals, idx = jax.lax.top_k(logits, K)
            gates = jax.nn.softmax(vals, axis=-1)
            N = x.shape[0] * x.shape[1]
            hf = h.reshape(N, D)
            h1 = jax.nn.gelu(jnp.einsum('nd,efd->enf', hf, fc1_w) + fc1_b[:, None, :], approximate=False)
            eo = jnp.einsum('enf,edf->end', h1, fc2_w) + fc2_b[:, None, :]
            idx_f = idx.reshape(N, K)
            gates_f = gates.reshape(N, K)
            gathered = eo[idx_f, jnp.arange(N)[:, None], :]
            mixed = (gathered * gates_f[..., None]).sum(axis=1).reshape(x.shape)
            return x + mixed
        key = jax.random.key(seed)
        ks = jax.random.split(key, 16)
        inp = {'latents': jax.random.normal(ks[0], (B, L, D), jnp.float32), 'tokens': jax.random.normal(ks[1], (B, T, D), jnp.float32), 'sa_ln_g': jnp.ones((D,)), 'sa_ln_b': jnp.zeros((D,)), 'sa_in_w': _xavier(ks[2], (3 * D, D)), 'sa_in_b': jnp.zeros((3 * D,)), 'sa_out_w': _xavier(ks[3], (D, D)), 'sa_out_b': jnp.zeros((D,)), 'ca_q_ln_g': jnp.ones((D,)), 'ca_q_ln_b': jnp.zeros((D,)), 'ca_kv_ln_g': jnp.ones((D,)), 'ca_kv_ln_b': jnp.zeros((D,)), 'ca_in_w': _xavier(ks[4], (3 * D, D)), 'ca_in_b': jnp.zeros((3 * D,)), 'ca_out_w': _xavier(ks[5], (D, D)), 'ca_out_b': jnp.zeros((D,)), 'moe_ln_g': jnp.ones((D,)), 'moe_ln_b': jnp.zeros((D,)), 'router_w': _xavier(ks[6], (E, D)), 'router_b': jnp.zeros((E,)), 'e_fc1_w': jax.vmap(lambda k: _xavier(k, (DFF, D)))(jax.random.split(ks[7], E)), 'e_fc1_b': jnp.zeros((E, DFF)), 'e_fc2_w': jax.vmap(lambda k: _xavier(k, (D, DFF)))(jax.random.split(ks[8], E)), 'e_fc2_b': jnp.zeros((E, D))}
        return inp
    _L0_xattn_all = _L0_xattn_setup()
    _L0_xattn_in = {k: v for k, v in _L0_xattn_all.items() if k in ('sa_ln_g', 'sa_ln_b', 'sa_in_w', 'sa_in_b', 'sa_out_w', 'sa_out_b', 'ca_q_ln_g', 'ca_q_ln_b', 'ca_kv_ln_g', 'ca_kv_ln_b', 'ca_in_w', 'ca_in_b', 'ca_out_w', 'ca_out_b', 'moe_ln_g', 'moe_ln_b', 'router_w', 'router_b', 'e_fc1_w', 'e_fc1_b', 'e_fc2_w', 'e_fc2_b')}
    del _L0_xattn_all

    def _L1_xattn_setup():
        import jax, jax.numpy as jnp
        import numpy as np
        B, S, SE, D, H, FF, E, K = (2, 256, 256, 128, 16, 512, 8, 2)
        HD = D // H

        def _layernorm(x, g, b):
            m = x.mean(-1, keepdims=True)
            v = ((x - m) ** 2).mean(-1, keepdims=True)
            return (x - m) / jnp.sqrt(v + 1e-05) * g + b

        def _attn(q_in, k_in, v_in, wq, bq, wk, bk, wv, bv, wo, bo, causal):
            Bq, Sq, Dm = q_in.shape
            Sk = k_in.shape[1]
            Q = (q_in @ wq + bq).reshape(Bq, Sq, H, HD)
            Kp = (k_in @ wk + bk).reshape(Bq, Sk, H, HD)
            V = (v_in @ wv + bv).reshape(Bq, Sk, H, HD)
            scores = jnp.einsum('bqhd,bkhd->bhqk', Q, Kp) / jnp.sqrt(jnp.float32(HD))
            if causal:
                mask = jnp.tril(jnp.ones((Sq, Sk), bool))
                scores = jnp.where(mask, scores, -jnp.inf)
            a = jax.nn.softmax(scores, axis=-1)
            o = jnp.einsum('bhqk,bkhd->bqhd', a, V).reshape(Bq, Sq, Dm)
            return o @ wo + bo

        def _moe(x, rw, rb, w1, b1, w2, b2):
            T = x.shape[0] * x.shape[1]
            xf = x.reshape(T, D)
            router_weights = jax.nn.softmax(xf @ rw + rb, axis=-1)
            topw, topi = jax.lax.top_k(router_weights, K)
            topw = jax.nn.softmax(topw, axis=-1)
            combine = jnp.zeros((T, E), xf.dtype).at[jnp.arange(T)[:, None], topi].add(topw)
            h = jax.nn.gelu(jnp.einsum('td,edf->etf', xf, w1) + b1[:, None, :], approximate=False)
            eo = jnp.einsum('etf,efd->etd', h, w2) + b2[:, None, :]
            out = jnp.einsum('etd,te->td', eo, combine)
            return out.reshape(x.shape)
        key = jax.random.key(seed)
        ks = jax.random.split(key, 32)
        w = lambda k, shape: jax.random.normal(k, shape, jnp.float32) * 0.02
        inp = {'x': jax.random.normal(ks[0], (B, S, D), jnp.float32), 'encoder_output': jax.random.normal(ks[1], (B, SE, D), jnp.float32), 'sa_wq': w(ks[2], (D, D)), 'sa_bq': jnp.zeros((D,), jnp.float32), 'sa_wk': w(ks[3], (D, D)), 'sa_bk': jnp.zeros((D,), jnp.float32), 'sa_wv': w(ks[4], (D, D)), 'sa_bv': jnp.zeros((D,), jnp.float32), 'sa_wo': w(ks[5], (D, D)), 'sa_bo': jnp.zeros((D,), jnp.float32), 'ca_wq': w(ks[6], (D, D)), 'ca_bq': jnp.zeros((D,), jnp.float32), 'ca_wk': w(ks[7], (D, D)), 'ca_bk': jnp.zeros((D,), jnp.float32), 'ca_wv': w(ks[8], (D, D)), 'ca_bv': jnp.zeros((D,), jnp.float32), 'ca_wo': w(ks[9], (D, D)), 'ca_bo': jnp.zeros((D,), jnp.float32), 'ln1_g': jnp.ones((D,), jnp.float32), 'ln1_b': jnp.zeros((D,), jnp.float32), 'ln2_g': jnp.ones((D,), jnp.float32), 'ln2_b': jnp.zeros((D,), jnp.float32), 'ln3_g': jnp.ones((D,), jnp.float32), 'ln3_b': jnp.zeros((D,), jnp.float32), 'router_w': w(ks[10], (D, E)), 'router_b': jnp.zeros((E,), jnp.float32), 'e_w1': w(ks[11], (E, D, FF)), 'e_b1': jnp.zeros((E, FF), jnp.float32), 'e_w2': w(ks[12], (E, FF, D)), 'e_b2': jnp.zeros((E, D), jnp.float32)}
        return inp
    _L1_xattn_all = _L1_xattn_setup()
    _L1_xattn_in = {k: v for k, v in _L1_xattn_all.items() if k in ('sa_wq', 'sa_bq', 'sa_wk', 'sa_bk', 'sa_wv', 'sa_bv', 'sa_wo', 'sa_bo', 'ca_wq', 'ca_bq', 'ca_wk', 'ca_bk', 'ca_wv', 'ca_bv', 'ca_wo', 'ca_bo', 'ln1_g', 'ln1_b', 'ln2_g', 'ln2_b', 'ln3_g', 'ln3_b', 'router_w', 'router_b', 'e_w1', 'e_b1', 'e_w2', 'e_b2')}
    del _L1_xattn_all
    return {'x': x, 'ctx_1024': ctx_1024, 'L0_xattn_sa_ln_g': _L0_xattn_in['sa_ln_g'], 'L0_xattn_sa_ln_b': _L0_xattn_in['sa_ln_b'], 'L0_xattn_sa_in_w': _L0_xattn_in['sa_in_w'], 'L0_xattn_sa_in_b': _L0_xattn_in['sa_in_b'], 'L0_xattn_sa_out_w': _L0_xattn_in['sa_out_w'], 'L0_xattn_sa_out_b': _L0_xattn_in['sa_out_b'], 'L0_xattn_ca_q_ln_g': _L0_xattn_in['ca_q_ln_g'], 'L0_xattn_ca_q_ln_b': _L0_xattn_in['ca_q_ln_b'], 'L0_xattn_ca_kv_ln_g': _L0_xattn_in['ca_kv_ln_g'], 'L0_xattn_ca_kv_ln_b': _L0_xattn_in['ca_kv_ln_b'], 'L0_xattn_ca_in_w': _L0_xattn_in['ca_in_w'], 'L0_xattn_ca_in_b': _L0_xattn_in['ca_in_b'], 'L0_xattn_ca_out_w': _L0_xattn_in['ca_out_w'], 'L0_xattn_ca_out_b': _L0_xattn_in['ca_out_b'], 'L0_xattn_moe_ln_g': _L0_xattn_in['moe_ln_g'], 'L0_xattn_moe_ln_b': _L0_xattn_in['moe_ln_b'], 'L0_xattn_router_w': _L0_xattn_in['router_w'], 'L0_xattn_router_b': _L0_xattn_in['router_b'], 'L0_xattn_e_fc1_w': _L0_xattn_in['e_fc1_w'], 'L0_xattn_e_fc1_b': _L0_xattn_in['e_fc1_b'], 'L0_xattn_e_fc2_w': _L0_xattn_in['e_fc2_w'], 'L0_xattn_e_fc2_b': _L0_xattn_in['e_fc2_b'], 'L1_xattn_sa_wq': _L1_xattn_in['sa_wq'], 'L1_xattn_sa_bq': _L1_xattn_in['sa_bq'], 'L1_xattn_sa_wk': _L1_xattn_in['sa_wk'], 'L1_xattn_sa_bk': _L1_xattn_in['sa_bk'], 'L1_xattn_sa_wv': _L1_xattn_in['sa_wv'], 'L1_xattn_sa_bv': _L1_xattn_in['sa_bv'], 'L1_xattn_sa_wo': _L1_xattn_in['sa_wo'], 'L1_xattn_sa_bo': _L1_xattn_in['sa_bo'], 'L1_xattn_ca_wq': _L1_xattn_in['ca_wq'], 'L1_xattn_ca_bq': _L1_xattn_in['ca_bq'], 'L1_xattn_ca_wk': _L1_xattn_in['ca_wk'], 'L1_xattn_ca_bk': _L1_xattn_in['ca_bk'], 'L1_xattn_ca_wv': _L1_xattn_in['ca_wv'], 'L1_xattn_ca_bv': _L1_xattn_in['ca_bv'], 'L1_xattn_ca_wo': _L1_xattn_in['ca_wo'], 'L1_xattn_ca_bo': _L1_xattn_in['ca_bo'], 'L1_xattn_ln1_g': _L1_xattn_in['ln1_g'], 'L1_xattn_ln1_b': _L1_xattn_in['ln1_b'], 'L1_xattn_ln2_g': _L1_xattn_in['ln2_g'], 'L1_xattn_ln2_b': _L1_xattn_in['ln2_b'], 'L1_xattn_ln3_g': _L1_xattn_in['ln3_g'], 'L1_xattn_ln3_b': _L1_xattn_in['ln3_b'], 'L1_xattn_router_w': _L1_xattn_in['router_w'], 'L1_xattn_router_b': _L1_xattn_in['router_b'], 'L1_xattn_e_w1': _L1_xattn_in['e_w1'], 'L1_xattn_e_b1': _L1_xattn_in['e_b1'], 'L1_xattn_e_w2': _L1_xattn_in['e_w2'], 'L1_xattn_e_b2': _L1_xattn_in['e_b2']}

def reference(x, ctx_1024, L0_xattn_sa_ln_g, L0_xattn_sa_ln_b, L0_xattn_sa_in_w, L0_xattn_sa_in_b, L0_xattn_sa_out_w, L0_xattn_sa_out_b, L0_xattn_ca_q_ln_g, L0_xattn_ca_q_ln_b, L0_xattn_ca_kv_ln_g, L0_xattn_ca_kv_ln_b, L0_xattn_ca_in_w, L0_xattn_ca_in_b, L0_xattn_ca_out_w, L0_xattn_ca_out_b, L0_xattn_moe_ln_g, L0_xattn_moe_ln_b, L0_xattn_router_w, L0_xattn_router_b, L0_xattn_e_fc1_w, L0_xattn_e_fc1_b, L0_xattn_e_fc2_w, L0_xattn_e_fc2_b, L1_xattn_sa_wq, L1_xattn_sa_bq, L1_xattn_sa_wk, L1_xattn_sa_bk, L1_xattn_sa_wv, L1_xattn_sa_bv, L1_xattn_sa_wo, L1_xattn_sa_bo, L1_xattn_ca_wq, L1_xattn_ca_bq, L1_xattn_ca_wk, L1_xattn_ca_bk, L1_xattn_ca_wv, L1_xattn_ca_bv, L1_xattn_ca_wo, L1_xattn_ca_bo, L1_xattn_ln1_g, L1_xattn_ln1_b, L1_xattn_ln2_g, L1_xattn_ln2_b, L1_xattn_ln3_g, L1_xattn_ln3_b, L1_xattn_router_w, L1_xattn_router_b, L1_xattn_e_w1, L1_xattn_e_b1, L1_xattn_e_w2, L1_xattn_e_b2):
    import jax
    import jax.numpy as jnp

    def _L0_xattn_ref(latents, tokens, sa_ln_g, sa_ln_b, sa_in_w, sa_in_b, sa_out_w, sa_out_b, ca_q_ln_g, ca_q_ln_b, ca_kv_ln_g, ca_kv_ln_b, ca_in_w, ca_in_b, ca_out_w, ca_out_b, moe_ln_g, moe_ln_b, router_w, router_b, e_fc1_w, e_fc1_b, e_fc2_w, e_fc2_b):
        import jax, jax.numpy as jnp
        import numpy as np
        D, H, E, K, DFF = (128, 16, 8, 2, 512)
        B, L, T = (4, 64, 256)
        EPS = 1e-05

        def _xavier(key, shape):
            fan_in, fan_out = (shape[-1], shape[-2])
            a = jnp.sqrt(6.0 / (fan_in + fan_out))
            return jax.random.uniform(key, shape, jnp.float32, -a, a)

        def _ln(x, g, b):
            m = x.mean(-1, keepdims=True)
            v = ((x - m) ** 2).mean(-1, keepdims=True)
            return (x - m) / jnp.sqrt(v + EPS) * g + b

        def _mha(q_in, kv_in, in_w, in_b, out_w, out_b):
            wq, wk, wv = jnp.split(in_w, 3, axis=0)
            bq, bk, bv = jnp.split(in_b, 3, axis=0)
            dh = D // H

            def heads(x, w, b):
                y = x @ w.T + b
                return y.reshape(x.shape[0], x.shape[1], H, dh).transpose(0, 2, 1, 3)
            q = heads(q_in, wq, bq)
            k = heads(kv_in, wk, bk)
            v = heads(kv_in, wv, bv)
            scores = jnp.einsum('bhqd,bhkd->bhqk', q, k) / jnp.sqrt(jnp.float32(dh))
            attn = jax.nn.softmax(scores, axis=-1)
            out = jnp.einsum('bhqk,bhkd->bhqd', attn, v)
            out = out.transpose(0, 2, 1, 3).reshape(q_in.shape[0], q_in.shape[1], D)
            return out @ out_w.T + out_b

        def _fuse_moe(x, ln_g, ln_b, rw, rb, fc1_w, fc1_b, fc2_w, fc2_b):
            h = _ln(x, ln_g, ln_b)
            logits = h @ rw.T + rb
            vals, idx = jax.lax.top_k(logits, K)
            gates = jax.nn.softmax(vals, axis=-1)
            N = x.shape[0] * x.shape[1]
            hf = h.reshape(N, D)
            h1 = jax.nn.gelu(jnp.einsum('nd,efd->enf', hf, fc1_w) + fc1_b[:, None, :], approximate=False)
            eo = jnp.einsum('enf,edf->end', h1, fc2_w) + fc2_b[:, None, :]
            idx_f = idx.reshape(N, K)
            gates_f = gates.reshape(N, K)
            gathered = eo[idx_f, jnp.arange(N)[:, None], :]
            mixed = (gathered * gates_f[..., None]).sum(axis=1).reshape(x.shape)
            return x + mixed
        q = _ln(latents, sa_ln_g, sa_ln_b)
        x = latents + _mha(q, q, sa_in_w, sa_in_b, sa_out_w, sa_out_b)
        qc = _ln(x, ca_q_ln_g, ca_q_ln_b)
        kv = _ln(tokens, ca_kv_ln_g, ca_kv_ln_b)
        x = x + _mha(qc, kv, ca_in_w, ca_in_b, ca_out_w, ca_out_b)
        return _fuse_moe(x, moe_ln_g, moe_ln_b, router_w, router_b, e_fc1_w, e_fc1_b, e_fc2_w, e_fc2_b)

    def _L1_xattn_ref(x, encoder_output, sa_wq, sa_bq, sa_wk, sa_bk, sa_wv, sa_bv, sa_wo, sa_bo, ca_wq, ca_bq, ca_wk, ca_bk, ca_wv, ca_bv, ca_wo, ca_bo, ln1_g, ln1_b, ln2_g, ln2_b, ln3_g, ln3_b, router_w, router_b, e_w1, e_b1, e_w2, e_b2):
        import jax, jax.numpy as jnp
        import numpy as np
        B, S, SE, D, H, FF, E, K = (2, 256, 256, 128, 16, 512, 8, 2)
        HD = D // H

        def _layernorm(x, g, b):
            m = x.mean(-1, keepdims=True)
            v = ((x - m) ** 2).mean(-1, keepdims=True)
            return (x - m) / jnp.sqrt(v + 1e-05) * g + b

        def _attn(q_in, k_in, v_in, wq, bq, wk, bk, wv, bv, wo, bo, causal):
            Bq, Sq, Dm = q_in.shape
            Sk = k_in.shape[1]
            Q = (q_in @ wq + bq).reshape(Bq, Sq, H, HD)
            Kp = (k_in @ wk + bk).reshape(Bq, Sk, H, HD)
            V = (v_in @ wv + bv).reshape(Bq, Sk, H, HD)
            scores = jnp.einsum('bqhd,bkhd->bhqk', Q, Kp) / jnp.sqrt(jnp.float32(HD))
            if causal:
                mask = jnp.tril(jnp.ones((Sq, Sk), bool))
                scores = jnp.where(mask, scores, -jnp.inf)
            a = jax.nn.softmax(scores, axis=-1)
            o = jnp.einsum('bhqk,bkhd->bqhd', a, V).reshape(Bq, Sq, Dm)
            return o @ wo + bo

        def _moe(x, rw, rb, w1, b1, w2, b2):
            T = x.shape[0] * x.shape[1]
            xf = x.reshape(T, D)
            router_weights = jax.nn.softmax(xf @ rw + rb, axis=-1)
            topw, topi = jax.lax.top_k(router_weights, K)
            topw = jax.nn.softmax(topw, axis=-1)
            combine = jnp.zeros((T, E), xf.dtype).at[jnp.arange(T)[:, None], topi].add(topw)
            h = jax.nn.gelu(jnp.einsum('td,edf->etf', xf, w1) + b1[:, None, :], approximate=False)
            eo = jnp.einsum('etf,efd->etd', h, w2) + b2[:, None, :]
            out = jnp.einsum('etd,te->td', eo, combine)
            return out.reshape(x.shape)
        x = _layernorm(x + _attn(x, x, x, sa_wq, sa_bq, sa_wk, sa_bk, sa_wv, sa_bv, sa_wo, sa_bo, True), ln1_g, ln1_b)
        x = _layernorm(x + _attn(x, encoder_output, encoder_output, ca_wq, ca_bq, ca_wk, ca_bk, ca_wv, ca_bv, ca_wo, ca_bo, False), ln2_g, ln2_b)
        x = _layernorm(x + _moe(x, router_w, router_b, e_w1, e_b1, e_w2, e_b2), ln3_g, ln3_b)
        return x
    x = _L0_xattn_ref(x, ctx_1024, L0_xattn_sa_ln_g, L0_xattn_sa_ln_b, L0_xattn_sa_in_w, L0_xattn_sa_in_b, L0_xattn_sa_out_w, L0_xattn_sa_out_b, L0_xattn_ca_q_ln_g, L0_xattn_ca_q_ln_b, L0_xattn_ca_kv_ln_g, L0_xattn_ca_kv_ln_b, L0_xattn_ca_in_w, L0_xattn_ca_in_b, L0_xattn_ca_out_w, L0_xattn_ca_out_b, L0_xattn_moe_ln_g, L0_xattn_moe_ln_b, L0_xattn_router_w, L0_xattn_router_b, L0_xattn_e_fc1_w, L0_xattn_e_fc1_b, L0_xattn_e_fc2_w, L0_xattn_e_fc2_b)
    x = _L1_xattn_ref(x, ctx_1024, L1_xattn_sa_wq, L1_xattn_sa_bq, L1_xattn_sa_wk, L1_xattn_sa_bk, L1_xattn_sa_wv, L1_xattn_sa_bv, L1_xattn_sa_wo, L1_xattn_sa_bo, L1_xattn_ca_wq, L1_xattn_ca_bq, L1_xattn_ca_wk, L1_xattn_ca_bk, L1_xattn_ca_wv, L1_xattn_ca_bv, L1_xattn_ca_wo, L1_xattn_ca_bo, L1_xattn_ln1_g, L1_xattn_ln1_b, L1_xattn_ln2_g, L1_xattn_ln2_b, L1_xattn_ln3_g, L1_xattn_ln3_b, L1_xattn_router_w, L1_xattn_router_b, L1_xattn_e_w1, L1_xattn_e_b1, L1_xattn_e_w2, L1_xattn_e_b2)
    return x

_drawn_inputs = setup_inputs


def setup_inputs(seed=0):
    import zlib

    import numpy as np

    out = dict(_drawn_inputs(seed))
    spreads = {'L0_xattn_sa_ln_g': (1.0, 0.2),
     'L0_xattn_sa_ln_b': (0.0, 0.1),
     'L0_xattn_sa_in_b': (0.0, 0.1),
     'L0_xattn_sa_out_b': (0.0, 0.1),
     'L0_xattn_ca_q_ln_g': (1.0, 0.2),
     'L0_xattn_ca_q_ln_b': (0.0, 0.296),
     'L0_xattn_ca_kv_ln_g': (1.0, 0.2),
     'L0_xattn_ca_kv_ln_b': (0.0, 0.1),
     'L0_xattn_ca_in_b': (0.0, 0.1),
     'L0_xattn_ca_out_b': (0.0, 0.1),
     'L0_xattn_moe_ln_g': (1.0, 0.2),
     'L0_xattn_moe_ln_b': (0.0, 0.1),
     'L0_xattn_router_b': (0.0, 0.1),
     'L0_xattn_e_fc1_b': (0.0, 0.1),
     'L0_xattn_e_fc2_b': (0.0, 0.1),
     'L1_xattn_sa_bq': (0.0, 2.0),
     'L1_xattn_sa_bk': (0.0, 2.0),
     'L1_xattn_sa_bv': (0.0, 0.465),
     'L1_xattn_sa_bo': (0.0, 0.1),
     'L1_xattn_ca_bq': (0.0, 2.0),
     'L1_xattn_ca_bk': (0.0, 2.0),
     'L1_xattn_ca_bv': (0.0, 0.296),
     'L1_xattn_ca_bo': (0.0, 0.1),
     'L1_xattn_ln1_g': (1.0, 0.2),
     'L1_xattn_ln1_b': (0.0, 0.1),
     'L1_xattn_ln2_g': (1.0, 0.2),
     'L1_xattn_ln2_b': (0.0, 0.1),
     'L1_xattn_ln3_g': (1.0, 0.2),
     'L1_xattn_ln3_b': (0.0, 0.1),
     'L1_xattn_router_b': (0.0, 0.1),
     'L1_xattn_e_b1': (0.0, 0.521),
     'L1_xattn_e_b2': (0.0, 0.1)}
    factors = {'L1_xattn_sa_wq': 8.0, 'L1_xattn_sa_wk': 8.0, 'L1_xattn_ca_wq': 8.0, 'L1_xattn_ca_wk': 8.0}
    for name, (base, spread) in spreads.items():
        noise = np.random.default_rng([zlib.crc32(name.encode()), seed]).standard_normal(out[name].shape)
        drawn = base * np.exp(spread * noise) if base else spread * noise
        out[name] = jnp.asarray(drawn.astype(out[name].dtype))
    for name, factor in factors.items():
        out[name] = (out[name] * factor).astype(out[name].dtype)
    return out
```

```python
import concourse.bass as bass
from concourse import mybir
from contextlib import ExitStack

B, S, D, H, HD, E, F, SE = 2, 512, 128, 16, 8, 8, 512, 77
NT = S // 128
SP = SE + 1
GH = 4
NG = H // GH
NC = F // 128
EPS = 1e-5
BIG = 1e30
ATT = 2 * NG * 128 + 2 * 128
COL_BQ, COL_BK = 0, 16
COL_LN = 32
COL_B1 = 44
COL_B2 = COL_B1 + 2 * E * NC
COL_QLO, COL_KLO = COL_B2 + 2 * E, COL_B2 + 2 * E + 1
COL_BQL = COL_KLO + 1
COL_BKL = COL_BQL + 16
COL_EPS = COL_BKL + 16
COL_ONE = COL_EPS + 1
COL_RW = COL_ONE + 1
COL_RB = COL_RW + 2 * E
COL_DESC = COL_RB + 2 * E
NCOL = COL_DESC + E
LN_SA, LN_CAQ, LN_CTX, LN_MOE, LN_1, LN_2 = range(6)
ROW_BV, ROW_BO, ROW_LN = 0, 4, 8
NROW = 14
KRING, QRING, PRING = 3, 3, 6
WSLOT = 4


def causal(n):
    return n in (4, 5)


def is_self(n):
    return n % 4 < 2


def att_of(n):
    return n // 2


MOE, LAST = 10, 20


def goal(n):
    return n + 2 if is_self(n) else MOE + 2 * (n // 4) + n % 2


def n_units(n):
    return 2 * NT if is_self(n) else 2


def n_max(n):
    return GH * NT if is_self(n) else NT


def make_plan():
    plan = []
    for L in range(2):
        first = 16 * L
        last = first + 15
        done = set()
        pending = []

        def emit(step):
            plan.append(step)
            done.add(step)

        def flush(pos):
            while pending and pending[0][0] <= pos:
                emit(pending.pop(0)[1])

        def need(step):
            while step not in done:
                emit(pending.pop(0)[1])

        def project(G):
            n = G // NG
            need(("turn", n))
            emit(("proj", G, "q"))
            if is_self(n):
                emit(("proj", G, "k"))

        def maxes(G, half):
            m = n_max(G // NG)
            return [("max", G, i) for i in range(m // 2 * half, m // 2 * (half + 1))]

        if L == 0:
            emit(("norm", 0)), emit(("norm", 1)), emit(("norm", "ctx"))
        for n in (4 * L, 4 * L + 1):
            emit(("turn", n))
            emit(("resid", n))
        for e in range(WSLOT if L == 0 else 0):
            emit(("wload", L, e))
        project(first)
        emit(("vproj", 4 * L))
        project(first + 1), project(first + 2)
        for s in maxes(first, 0) + maxes(first, 1):
            emit(s)
        emit(("mt", first))
        for s in maxes(first + 1, 0):
            emit(s)
        pos = 0
        for G in range(first, last + 1):
            n, g = divmod(G, NG)
            U = n_units(n)
            side = [[], []]
            if G + 1 <= last:
                side[0] += maxes(G + 1, 1) + [("mt", G + 1)]
            if G + 3 <= last:
                side[1] += [("project", G + 3)]
            if n % 4 == 0 and g == 1:
                side[0] += [("vproj", n + 1)]
            if n % 4 == 0:
                side[1] += [("cproj", L, g)]
                if g == 0:
                    side[0] = [("cturn", L)] + side[0]
                    side[1] += [("cvproj", L)]
            if L == 0 and n == 0 or L == 1 and n == 4:
                side[1] += [("wsplit", L, g)]
            if G + 2 <= last:
                side[1] += maxes(G + 2, 0)
            for half in range(2):
                todo = side[half]
                steps = U // 2
                for u in range(steps):
                    emit(("unit", G, half * steps + u))
                    if (half * steps + u) % 2:
                        kb = (half * steps + u) // 2
                        pending.append((pos + 2, ("av", G, kb)))
                        if kb == U // 2 - 1:
                            pending.append((pos + 2, ("oev", G)))
                            pending.append((pos + 4, ("otr", G)))
                            if g == NG - 1:
                                pending += [(pos + 5, ("aturn", n)), (pos + 5, ("oproj", n))]
                                pending += [(pos + 5, (s, goal(n))) for s in ("norm", "turn", "resid")
                                            if s != "resid" or goal(n) not in (MOE, MOE + 1)]
                                if L == 0 and n % 2:
                                    pending.append((pos + 5, ("watt", 2 + n // 2)))
                        pending.sort(key=lambda t: t[0])
                    flush(pos)
                    k = len(todo) * (u + 1) // steps - len(todo) * u // steps
                    for s in todo[len(todo) * u // steps:][:k]:
                        if s[0] == "project":
                            project(s[1])
                        else:
                            emit(s)
                    pos += 1
        flush(10 ** 9)
        for b in range(B):
            emit(("route", L, b))
        emit(("fc1", L, 0))
        for k in range(2 * E):
            emit(("cbc", L, k))
            if k + 1 < 2 * E:
                emit(("fc1", L, k + 1))
            emit(("fc2", L, k))
            e = k // 2
            if k % 2 == 1:
                nL, ne = divmod(L * E + e + WSLOT, E)
                if nL < 2:
                    emit(("wload", nL, ne))
                    if nL == L:
                        emit(("wsplit", nL, ne))
        for b in range(B):
            emit(("mout", L, b))
        if L == 1:
            for b in range(B):
                emit(("norm", LAST + b)), emit(("final", b))
    return plan


PLAN = make_plan()
ORD, _seen = {}, {}
for _s in PLAN:
    ORD[_s] = _seen.get(_s[0], 0)
    _seen[_s[0]] = ORD[_s] + 1
THROUGH_MISC = ("proj", "cproj", "vproj", "cvproj", "mt", "otr", "aturn", "oproj", "turn", "cturn", "route", "mout")
MISC = {s: i for i, s in enumerate(s for s in PLAN if s[0] in THROUGH_MISC)}
SPLIT = {s: i for i, s in enumerate(s for s in PLAN if s[0] in ("proj", "cproj"))}
KOUT = [s for s in SPLIT if s[0] == "cproj" or s[2] == "k"]
MAX = {s: i for i, s in enumerate(s for s in PLAN if s[0] == "max")}
SELFG = [G for G in range(32) if is_self(G // NG)]


def build(nc, x_in, ctx_in, watt_in, cols_in, rows_in, w_in, out):
    f32, f32r = mybir.dt.float32, mybir.dt.float32r
    ALU = mybir.AluOpType
    ACT = mybir.ActivationFunctionType
    AX = mybir.AxisListType

    ctx = ExitStack()
    with ctx:
        def sb(name, shape, dt=f32):
            return ctx.enter_context(nc.sbuf_tensor(name, shape, dt))

        def sem(name):
            return ctx.enter_context(nc.semaphore(name))

        ident = sb("ident", [128, 128])
        ident_r = sb("ident_r", [128, 128], f32r)
        mask = sb("mask", [128, 2, 128])
        mask_r = sb("mask_r", [128, 2, 128], f32r)
        cols = sb("cols", [128, NCOL])
        rows = sb("rows", [128, NROW, 128])
        watt = [sb(f"watt{i}", [128, ATT]) for i in range(2)]
        x = [sb(f"x{b}", [128, NT, 128]) for b in range(B)]
        res = [sb(f"res{b}", [128, NT, 128]) for b in range(B)]
        xhat = [sb(f"xhat{b}", [128, NT, 128]) for b in range(B)]
        hT = [sb(f"hT{b}", [128, S]) for b in range(B)]
        hT_hi = [sb(f"hT_hi{b}", [128, S], f32r) for b in range(B)]
        hT_lo = [sb(f"hT_lo{b}", [128, S], f32r) for b in range(B)]
        ctx_x = sb("ctx_x", [SE, B, 128])
        ctx_hat = sb("ctx_hat", [SE, B, 128])
        ctxT = sb("ctxT", [128, B, SP])
        stats = sb("stats", [128, 3, NT, 6])
        mv = sb("mv", [128, 3, NT, 2])
        rstd = sb("rstd", [128, 3, 4, NT])
        split_y = [sb(f"split_y{i}", [128, S]) for i in range(2)]
        split_hi = [sb(f"split_hi{i}", [128, S], f32r) for i in range(2)]
        k_out = [sb(f"k_out{i}", [128, S], f32r) for i in range(2)]
        q_st = [sb(f"q_st{i}", [128, S], f32r) for i in range(QRING)]
        q_max = [sb(f"q_max{i}", [128, S], f32r) for i in range(2)]
        k_m = [sb(f"k_m{i}", [128, GH, S], f32r) for i in range(KRING)]
        kc_m = sb("kc_m", [128, NG, GH, B * SP], f32r)
        v_aug = [sb(f"v_aug{i}", [128, NT, H, 32]) for i in range(2)]
        vc_aug = sb("vc_aug", [SE, B, H, 32])
        m_raw = [sb(f"m_raw{i}", [128, NT, GH]) for i in range(2)]
        m_cols = sb("m_cols", [128, NT, 128])
        P = [sb(f"P{i}", [128, 2, S]) for i in range(PRING)]
        o_sb = [sb(f"o_sb{i}", [128, S]) for i in range(2)]
        rden = sb("rden", [128, NT * GH])
        a_tok = [sb(f"a_tok{b}", [128, NT, 128]) for b in range(B)]
        aT = sb("aT", [128, S])
        w_hi = [sb(f"w_hi{i}", [128, F], f32r) for i in range(WSLOT)]
        w_lo = [sb(f"w_lo{i}", [128, F], f32r) for i in range(WSLOT)]
        w2 = [sb(f"w2{i}", [128, NC * 128]) for i in range(WSLOT)]
        w_raw = [sb(f"w_raw{i}", [128, F]) for i in range(WSLOT)]
        r = sb("r", [128, 7, NT, E])
        rs = sb("rs", [128, 9, NT])
        comb = [sb(f"comb{b}", [128, NT, E]) for b in range(B)]
        gate_bc = [sb(f"gate_bc{i}", [128, S]) for i in range(2)]
        eo = [sb(f"eo{i}", [128, S]) for i in range(2)]
        acc = [sb(f"acc{b}", [128, S]) for b in range(B)]

        ps_max = [ctx.enter_context(nc.psum_tensor(f"ps_max{i}", [128, S], f32)) for i in range(2)]
        ps_sc = [ctx.enter_context(nc.psum_tensor(f"ps_sc{i}", [128, 2, S], f32)) for i in range(2)]
        ps_o = ctx.enter_context(nc.psum_tensor("ps_o", [128, S], f32))
        ps_misc = ctx.enter_context(nc.psum_tensor("ps_misc", [128, S], f32))

        misc_written, misc_done = sem("misc_written"), sem("misc_done")
        consts_loaded, x_loaded, ctx_loaded = sem("consts_loaded"), sem("x_loaded"), sem("ctx_loaded")
        rows_loaded = sem("rows_loaded")
        watt_loaded = [sem("watt_loaded0"), sem("watt_loaded1")]
        ident_ready, masks_ready, pads_ready = sem("ident_ready"), sem("masks_ready"), sem("pads_ready")
        vpads_ready, rows_ready = sem("vpads_ready"), sem("rows_ready")
        var_ready, rstd_raw, xhat_ready = sem("var_ready"), sem("rstd_raw"), sem("xhat_ready")
        stack_ready, hlo_ready, res_ready = sem("stack_ready"), sem("hlo_ready"), sem("res_ready")
        k_moved = [sem(f"k_moved{i}") for i in range(KRING)]
        kc_moved = sem("kc_moved")
        max_written, max_read, mcols_ready = sem("max_written"), sem("max_read"), sem("mcols_ready")
        scores_written, probs_ready, av_done = sem("scores_written"), sem("probs_ready"), sem("av_done")
        o_ready = sem("o_ready")
        w_loaded = [sem(f"w_loaded{i}") for i in range(WSLOT)]
        w_split = sem("w_split")
        exp_in, exp_out, comb_ready = sem("exp_in"), sem("exp_out"), sem("comb_ready")
        fc1_written, hidden_ready, fc2_written, fc2_read = (
            sem("fc1_written"), sem("hidden_ready"), sem("fc2_written"), sem("fc2_read"))
        gate_written, gate_ready, acc_added = sem("gate_written"), sem("gate_ready"), sem("acc_added")
        final_ready, stored = sem("final_ready"), sem("stored")
        dve_chain, act_chain, pool_chain = sem("dve_chain"), sem("act_chain"), sem("pool_chain")

        def col(i, p=128):
            return cols[0:p, i:i + 1]

        def row(i, p=128, n=NT):
            return rows[0:p, i, :].unsqueeze(1).to_broadcast([p, n, 128])

        def over_tiles(ap):
            return ap.unsqueeze(1).to_broadcast([128, NT, E])

        def over_experts(ap):
            return ap.unsqueeze(2).to_broadcast([128, NT, E])

        def kslot(G):
            return SELFG.index(G) % KRING

        def kuse(G):
            return SELFG.index(G) // KRING + 1

        def avs_before(G):
            return sum(n_units(g // NG) // 2 for g in range(G))

        def units_before(G):
            return sum(n_units(g // NG) for g in range(G))

        def maxes_before(G):
            return sum(n_max(g // NG) for g in range(G))

        UNIT_GROUP = [(G, u) for G in range(32) for u in range(n_units(G // NG))]

        def hidden(k, c):
            return P[(2 * k) % PRING + c // 2][:, c % 2, :]

        def fc1_bank(f):
            return ps_sc[f % 4 // 2][:, f % 2, :]

        def q0_of(G, kb):
            return kb * 128 if causal(G // NG) else 0

        block = ctx.enter_context(nc.Block())

        @block.sync
        def _(sp):
            sp.dma_start(x[0][:, :, :], x_in[:, 0, :, :]).then_inc(x_loaded, 16)
            sp.dma_start(cols[:, :], cols_in).then_inc(consts_loaded, 16)
            sp.dma_start(watt[0][:, :], watt_in[0]).then_inc(watt_loaded[0], 16)
            sp.dma_start(x[1][:, :, :], x_in[:, 1, :, :]).then_inc(x_loaded, 16)
            sp.dma_start(ctx_x[:, :, :], ctx_in).then_inc(ctx_loaded, 16)
            sp.dma_start(rows[:, :, :], rows_in.unsqueeze(0).to_broadcast([128, NROW, 128])).then_inc(rows_loaded, 16)
            sp.dma_start(watt[1][:, :], watt_in[1]).then_inc(watt_loaded[1], 16)
            sp.wait_ge(pads_ready, 1)
            for s in PLAN:
                if s[0] == "watt":
                    a = s[1]
                    sp.wait_ge(misc_written, MISC[("oproj", 2 * (a - 2) + 1)] + 1)
                    sp.dma_start(watt[a % 2][:, :], watt_in[a]).then_inc(watt_loaded[a % 2], 16)
                elif s[0] == "proj" and s[2] == "k":
                    G = s[1]
                    sp.wait_ge(stack_ready, SPLIT[s] + 1)
                    if kuse(G) > 1:
                        sp.wait_ge(scores_written, units_before(SELFG[SELFG.index(G) - KRING] + 1))
                    for j in range(GH):
                        p = slice(32 * j, 32 * j + 32)
                        sp.dma_start(k_m[kslot(G)][p, j, :].bitcast(f32),
                                     k_out[KOUT.index(s) % 2][p, :].bitcast(f32)).then_inc(k_moved[kslot(G)], 16)
                elif s[0] == "cproj":
                    L, g = s[1], s[2]
                    sp.wait_ge(stack_ready, SPLIT[s] + 1)
                    if L == 1:
                        sp.wait_ge(scores_written, units_before(16))
                    for j in range(GH):
                        p = slice(32 * j, 32 * j + 32)
                        sp.dma_start(kc_m[p, g, j, :].bitcast(f32),
                                     k_out[KOUT.index(s) % 2][p, 0:B * SP].bitcast(f32)).then_inc(kc_moved, 16)
                elif s[0] == "wload":
                    L, e = s[1], s[2]
                    k = L * E + e
                    if k >= WSLOT:
                        sp.wait_ge(fc2_written, 2 * (k - WSLOT + 1))
                        sp.wait_ge(w_split, 2 * (k - WSLOT + 1))
                    sp.dma_start(w_raw[k % WSLOT][:, :], w_in[k, :, 0:F]).then_inc(w_loaded[k % WSLOT], 16)
                    sp.dma_start(w2[k % WSLOT][:, :], w_in[k, :, F:2 * F]).then_inc(w_loaded[k % WSLOT], 16)
                elif s[0] == "final":
                    b = s[1]
                    sp.wait_ge(final_ready, b + 1)
                    sp.dma_start(out[:, b, :, :], res[b][:, :, :]).then_inc(stored, 16)
            sp.wait_ge(stored, 16 * B)

        @block.gpsimd
        def _(pool):
            chain = [0]

            def link(ins):
                chain[0] += 1
                ins.then_inc(pool_chain, 1)
                pool.wait_ge(pool_chain, chain[0])

            link(pool.memset(ident[:, :], 0.0))
            pool.affine_select(out=ident[:, :], in_=ident[:, :], compare_op=ALU.not_equal, fill=1.0, base=0,
                               pattern=[[-1, 128]], channel_multiplier=1).then_inc(ident_ready, 1)
            pool.memset(ctxT[:, :, :], 0.0)
            for t in k_m:
                pool.memset(t[:, :, :].bitcast(f32), 0.0)
            pool.memset(kc_m[:, :, :, :].bitcast(f32), 0.0)
            pool.memset(m_cols[:, :, :], 0.0).then_inc(pads_ready, 1)
            link(pool.memset(mask[:, :, :], 0.0))
            pool.affine_select(out=mask[:, 0, :], in_=mask[:, 0, :], compare_op=ALU.is_ge, fill=-BIG, base=0,
                               pattern=[[-1, 128]], channel_multiplier=1)
            pool.affine_select(out=mask[:, 1, :], in_=mask[:, 1, :], compare_op=ALU.is_ge, fill=-BIG, base=0,
                               pattern=[[1, 128]], channel_multiplier=-1).then_inc(masks_ready, 1)
            pool.wait_ge(consts_loaded, 16)
            pool.wait_ge(rows_loaded, 16)
            pool.tensor_tensor(rows[:, ROW_LN + 1, :], rows[:, ROW_LN + 1, :], rows[:, ROW_BO + 3, :],
                               ALU.add).then_inc(rows_ready, 1)
            pool.wait_ge(rows_ready, 1)
            for s in PLAN:
                if s in SPLIT:
                    i = SPLIT[s]
                    w = S if s[0] == "proj" else B * SP
                    pool.wait_ge(misc_done, MISC[s] + 1)
                    if s[0] == "proj" and s[2] == "q":
                        G = s[1]
                        if G >= QRING:
                            pool.wait_ge(misc_done, MISC[("mt", G - QRING)] + 1)
                        dst = q_st[G % QRING]
                    else:
                        k = KOUT.index(s)
                        if k >= 2:
                            t = KOUT[k - 2]
                            if t[0] == "cproj":
                                pool.wait_ge(kc_moved, 64 * (ORD[t] + 1))
                            else:
                                pool.wait_ge(k_moved[kslot(t[1])], 64 * kuse(t[1]))
                        dst = k_out[k % 2]
                    pool.tensor_tensor(dst[:, 0:w], split_y[i % 2][:, 0:w], split_hi[i % 2][:, 0:w].bitcast(f32),
                                       ALU.subtract).then_inc(stack_ready, 1)
                elif s[0] == "resid":
                    d = s[1]
                    b = d % 2
                    if d < 6:
                        if d < 2:
                            pool.wait_ge(x_loaded, 16 * B)
                        else:
                            pool.wait_ge(misc_done, MISC[("oproj", d - 2) if d < 4 else ("mout", 0, b)] + 1)
                        pool.tensor_tensor(res[b][:, :, :], x[b][:, :, :], row(ROW_BO + d // 2),
                                           ALU.add).then_inc(res_ready, 1)
                    elif d in (6, 7, MOE + 2, MOE + 3):
                        r0 = ROW_LN + (0 if d < MOE else 2)
                        pool.wait_ge(xhat_ready, ORD[("norm", d)] + 1)
                        link(pool.tensor_tensor(res[b][:, :, :], xhat[b][:, :, :], row(r0), ALU.mult))
                        pool.tensor_tensor(res[b][:, :, :], res[b][:, :, :], row(r0 + 1),
                                           ALU.add).then_inc(res_ready, 1)
                elif s[0] == "turn" and s[1] >= MOE:
                    b = s[1] % 2
                    pool.wait_ge(misc_done, MISC[s] + 1)
                    pool.tensor_tensor(hT_lo[b][:, :], hT[b][:, :], hT_hi[b][:, :].bitcast(f32),
                                       ALU.subtract).then_inc(hlo_ready, 1)
                elif s[0] == "wsplit":
                    k = s[1] * E + s[2]
                    i = k % WSLOT
                    pool.wait_ge(w_loaded[i], 32 * (k // WSLOT + 1))
                    pool.tensor_copy(w_hi[i][:, :], w_raw[i][:, :]).then_inc(w_split, 1)
                    pool.wait_ge(w_split, 2 * k + 1)
                    pool.tensor_tensor(w_lo[i][:, :], w_raw[i][:, :], w_hi[i][:, :].bitcast(f32),
                                       ALU.subtract).then_inc(w_split, 1)
                elif s[0] == "fc2" and s[2] >= 2:
                    L, k = s[1], s[2]
                    b = k % 2
                    pool.wait_ge(fc2_read, 16 * L + k + 1)
                    if k >= 4:
                        pool.wait_ge(acc_added, 14 * L + k - 3)
                    pool.tensor_tensor(acc[b][:, :], acc[b][:, :], eo[k % 2][:, :], ALU.add).then_inc(acc_added, 1)

        @block.scalar
        def _(act):
            chain = [0]

            def link(ins):
                chain[0] += 1
                ins.then_inc(act_chain, 1)
                act.wait_ge(act_chain, chain[0])

            exps = 0
            act.wait_ge(consts_loaded, 16)
            for s in PLAN:
                if s in MISC:
                    reads = s[0] in ("proj", "cproj", "turn", "cturn", "aturn")
                    if reads:
                        act.wait_ge(misc_written, MISC[s] + 1)
                if s[0] == "norm":
                    i = 2 if s[1] == "ctx" else s[1] % 2
                    p, t = (SE, B) if s[1] == "ctx" else (128, NT)
                    act.wait_ge(var_ready, ORD[s] + 1)
                    link(act.activation(rstd[0:p, i, 0, 0:t], mv[0:p, i, 0:t, 1], ACT.Ln, bias=col(COL_EPS, p)))
                    act.activation(rstd[0:p, i, 1, 0:t], rstd[0:p, i, 0, 0:t], ACT.Exp, scale=-0.5).then_inc(rstd_raw, 1)
                elif s in SPLIT:
                    i = SPLIT[s]
                    n = s[1] // NG if s[0] == "proj" else 4 * s[1] + 2
                    g = s[1] % NG if s[0] == "proj" else s[2]
                    w = S if s[0] == "proj" else B * SP
                    a = 4 * (n // 2) + g
                    bias, bias_lo, lo = ((col(COL_BQ + a), col(COL_BQL + a), col(COL_QLO)) if s[-1] == "q" else
                                         (col(COL_BK + a), col(COL_BKL + a), col(COL_KLO)))
                    if i >= 2:
                        act.wait_ge(stack_ready, i - 1)
                    act.activation(split_y[i % 2][:, 0:w], ps_misc[:, 0:w], ACT.Identity, bias=bias)
                    act.activation(split_hi[i % 2][:, 0:w], ps_misc[:, 0:w], ACT.Identity,
                                   bias=bias_lo, scale=lo).then_inc(misc_done, 1)
                elif s[0] == "turn":
                    d = s[1]
                    b = d % 2
                    if d in (4, 5):
                        gain, shift = 1.0, 0.0
                    else:
                        ln = {0: LN_SA, 1: LN_CAQ, 3: LN_1, 5: LN_MOE, 6: LN_2}[d // 2]
                        gain, shift = col(COL_LN + 2 * ln), col(COL_LN + 2 * ln + 1)
                    if d >= MOE:
                        act.activation(hT_hi[b][:, :], ps_misc[:, :], ACT.Identity, bias=shift, scale=gain)
                    act.activation(hT[b][:, :], ps_misc[:, :], ACT.Identity, bias=shift,
                                   scale=gain).then_inc(misc_done, 1)
                elif s[0] == "cturn":
                    gain, shift = (col(COL_LN + 2 * LN_CTX), col(COL_LN + 2 * LN_CTX + 1)) if s[1] == 0 else (1.0, 0.0)
                    act.wait_ge(pads_ready, 1)
                    act.activation(ctxT[:, :, 0:SE], ps_misc[:, 0:B * SP].rearrange("p (b s) -> p b s", b=B)[:, :, 0:SE],
                                   ACT.Identity, bias=shift, scale=gain).then_inc(misc_done, 1)
                elif s[0] == "aturn":
                    act.activation(aT[:, :], ps_misc[:, :], ACT.Identity).then_inc(misc_done, 1)
                elif s[0] == "unit":
                    G, u = s[1], s[2]
                    t = units_before(G) + u
                    kb = u // 2
                    p = 128 if is_self(G // NG) else SE
                    w = S - q0_of(G, kb)
                    act.wait_ge(scores_written, t + 1)
                    if t - PRING >= units_before(16 * (G // 16)):
                        G2, u2 = UNIT_GROUP[t - PRING]
                        act.wait_ge(av_done, avs_before(G2) + u2 // 2 + 1)
                    elif G >= 16:
                        act.wait_ge(fc2_written, 16)
                    act.activation(P[t % PRING][0:p, :, 0:w], ps_sc[t % 2][0:p, :, 0:w], ACT.Exp,
                                   scale=float(HD) ** -0.5).then_inc(probs_ready, 1)
                elif s[0] == "oev":
                    G = s[1]
                    act.wait_ge(av_done, avs_before(G + 1))
                    if G >= 2:
                        act.wait_ge(misc_written, MISC[("otr", G - 2)] + 1)
                    act.activation(o_sb[G % 2][:, :], ps_o[:, :], ACT.Identity).then_inc(o_ready, 1)
                elif s[0] == "route":
                    for n in range(1 + s[1]):
                        exps += 1
                        act.wait_ge(exp_in, exps)
                        src, dst = (r[:, 1, :, :], r[:, 2, :, :]) if s[1] - n == 1 else (rs[:, 7, :], rs[:, 8, :])
                        act.activation(dst, src, ACT.Exp).then_inc(exp_out, 1)
                elif s[0] == "fc1":
                    L, k = s[1], s[2]
                    e = k // 2
                    if k < 3:
                        act.wait_ge(av_done, avs_before(16 * (L + 1)))
                    else:
                        act.wait_ge(fc2_written, 16 * L + k - 2)
                    for c in range(NC):
                        f = 64 * L + NC * k + c
                        act.wait_ge(fc1_written, f + 1)
                        act.activation(hidden(k, c), fc1_bank(f), ACT.Gelu,
                                       bias=col(COL_B1 + (L * E + e) * NC + c)).then_inc(hidden_ready, 1)
                elif s[0] == "cbc":
                    L, k = s[1], s[2]
                    act.wait_ge(gate_written, 16 * L + k + 1)
                    if k >= 2:
                        act.wait_ge(fc2_read, 16 * L + k - 1)
                    act.activation(gate_bc[k % 2][:, :], ps_o[:, :], ACT.Identity).then_inc(gate_ready, 1)

        @block.tensor
        def _(pe):
            def free_misc(s):
                if MISC[s]:
                    pe.wait_ge(misc_done, MISC[s])

            def turn_tiles(src, dst):
                for t in range(NT):
                    ins = pe.transpose(ps_misc[:, t * 128:(t + 1) * 128], src[:, t, :], dst)
                return ins

            def wait_attention_weights(a):
                pe.wait_ge(watt_loaded[a % 2], 16 * (a // 2 + 1))

            pe.wait_ge(consts_loaded, 16)
            pe.wait_ge(ident_ready, 1)
            for s in PLAN:
                if s in MISC:
                    free_misc(s)
                if s[0] == "turn":
                    d = s[1]
                    b = d % 2
                    if d in (4, 5):
                        pe.wait_ge(misc_done, MISC[("mout", 0, b)] + 1)
                        turn_tiles(x[b], ident[:, :]).then_inc(misc_written, 1)
                    else:
                        pe.wait_ge(xhat_ready, ORD[("norm", d)] + 1)
                        turn_tiles(xhat[b], ident[:, :]).then_inc(misc_written, 1)
                elif s[0] == "cturn":
                    src = ctx_hat if s[1] == 0 else ctx_x
                    if s[1] == 0:
                        pe.wait_ge(xhat_ready, ORD[("norm", "ctx")] + 1)
                    for b in range(B):
                        ins = pe.transpose(ps_misc[:, b * SP:b * SP + SE], src[:, b, :], ident[0:SE, 0:SE])
                    ins.then_inc(misc_written, 1)
                elif s[0] == "proj":
                    G = s[1]
                    n, g = divmod(G, NG)
                    wait_attention_weights(att_of(n))
                    pe.wait_ge(misc_done, MISC[("turn", n)] + 1)
                    c = g * 128 + (0 if s[2] == "q" else NG * 128)
                    pe.matmul(ps_misc[:, :], watt[att_of(n) % 2][:, c:c + 128], hT[n % 2][:, :],
                              start=True, stop=True).then_inc(misc_written, 1)
                elif s[0] == "cproj":
                    L, g = s[1], s[2]
                    wait_attention_weights(2 * L + 1)
                    c = (NG + g) * 128
                    pe.matmul(ps_misc[:, 0:B * SP], watt[1][:, c:c + 128], ctxT[:, :, :],
                              start=True, stop=True).then_inc(misc_written, 1)
                elif s[0] == "vproj":
                    n = s[1]
                    for t in range(NT):
                        ins = pe.matmul(ps_misc[:, t * 128:(t + 1) * 128], hT[n % 2][:, t * 128:(t + 1) * 128],
                                        watt[att_of(n) % 2][:, 1024:1152], start=True, stop=True)
                    ins.then_inc(misc_written, 1)
                elif s[0] == "cvproj":
                    for b in range(B):
                        ins = pe.matmul(ps_misc[0:SE, b * 128:(b + 1) * 128], ctxT[:, b, 0:SE],
                                        watt[1][:, 1024:1152], start=True, stop=True)
                    ins.then_inc(misc_written, 1)
                elif s[0] == "max":
                    G, i = s[1], s[2]
                    n, g = divmod(G, NG)
                    m = MAX[s]
                    if i == 0:
                        pe.wait_ge(stack_ready, SPLIT[("proj", G, "q")] + 1)
                        if is_self(n):
                            pe.wait_ge(k_moved[kslot(G)], 64 * kuse(G))
                        else:
                            pe.wait_ge(kc_moved, 256 * (n // 4 + 1))
                        if n >= 4:
                            pe.wait_ge(masks_ready, 2)
                    if m >= 2:
                        pe.wait_ge(max_read, m - 1)
                    if m == maxes_before(16):
                        pe.wait_ge(fc2_read, 16)
                    dst = ps_max[m % 2]
                    if is_self(n):
                        qb, j = divmod(i, GH)
                        q = q_st[G % QRING][:, qb * 128:(qb + 1) * 128]
                        w = (qb + 1) * 128 if causal(n) else S
                        ins = pe.matmul(dst[:, 0:w], q, k_m[kslot(G)][:, j, 0:w], start=True, stop=not causal(n))
                        if causal(n):
                            ins = pe.matmul(dst[:, w - 128:w], ident_r[:, :], mask_r[:, 0, :], start=False, stop=True)
                    else:
                        q = q_st[G % QRING][:, i * 128:(i + 1) * 128]
                        for j in range(GH):
                            ins = pe.matmul(dst[:, j * 128:j * 128 + SP], q,
                                            kc_m[:, g, j, (n % 2) * SP:(n % 2 + 1) * SP], start=True, stop=True)
                    ins.then_inc(max_written, 1)
                elif s[0] == "mt":
                    pe.wait_ge(mcols_ready, s[1] + 1)
                    turn_tiles(m_cols, ident[:, :]).then_inc(misc_written, 1)
                elif s[0] == "unit":
                    G, u = s[1], s[2]
                    n, g = divmod(G, NG)
                    t = units_before(G) + u
                    kb, pair = divmod(u, 2)
                    q0 = q0_of(G, kb)
                    if u == 0:
                        pe.wait_ge(misc_done, MISC[("mt", G)] + 1)
                    if t >= 2:
                        pe.wait_ge(probs_ready, t - 1)
                    if t == units_before(16):
                        pe.wait_ge(hidden_ready, 64)
                    for jj in range(2):
                        j = 2 * pair + jj
                        if is_self(n):
                            dst, k = ps_sc[t % 2][:, jj, 0:S - q0], k_m[kslot(G)][:, j, kb * 128:(kb + 1) * 128]
                        else:
                            dst = ps_sc[t % 2][0:SE, jj, :]
                            k = kc_m[:, g, j, (n % 2) * SP:(n % 2) * SP + SE]
                        ins = pe.matmul(dst, k, q_max[G % 2][:, q0:S], start=True, stop=not causal(n))
                        if causal(n):
                            ins = pe.matmul(ps_sc[t % 2][:, jj, 0:128], ident_r[:, :], mask_r[:, 1, :],
                                            start=False, stop=True)
                    ins.then_inc(scores_written, 1)
                elif s[0] == "av":
                    G, kb = s[1], s[2]
                    n, g = divmod(G, NG)
                    q0 = q0_of(G, kb)
                    w = S - q0
                    if kb == 0:
                        v = ("vproj", n) if is_self(n) else ("cvproj", n // 4)
                        pe.wait_ge(misc_done, MISC[v] + 1)
                        if G:
                            pe.wait_ge(o_ready, G)
                        if G == 16:
                            pe.wait_ge(gate_ready, 16)
                    t = units_before(G) + 2 * kb
                    pe.wait_ge(probs_ready, t + 2)
                    last = kb == n_units(n) // 2 - 1
                    for j in range(GH):
                        h = GH * g + j
                        if is_self(n):
                            v, pr = v_aug[n % 2][:, kb, h, :], P[(t + j // 2) % PRING][:, j % 2, 0:w]
                        else:
                            v, pr = vc_aug[:, n % 2, h, :], P[(t + j // 2) % PRING][0:SE, j % 2, :]
                        ins = pe.matmul(ps_o[32 * j:32 * j + 32, q0:S], v, pr, start=kb == 0, stop=last)
                    ins.then_inc(av_done, 1)
                elif s[0] == "otr":
                    G = s[1]
                    pe.wait_ge(o_ready, G + 1)
                    for t in range(NT):
                        ins = pe.transpose(ps_misc[:, t * 128:(t + 1) * 128], o_sb[G % 2][:, t * 128:(t + 1) * 128],
                                           ident[:, :])
                    ins.then_inc(misc_written, 1)
                elif s[0] == "aturn":
                    turn_tiles(a_tok[s[1] % 2], ident[:, :]).then_inc(misc_written, 1)
                elif s[0] == "oproj":
                    n = s[1]
                    for t in range(NT):
                        ins = pe.matmul(ps_misc[:, t * 128:(t + 1) * 128], aT[:, t * 128:(t + 1) * 128],
                                        watt[att_of(n) % 2][:, 1152:1280], start=True, stop=True)
                    ins.then_inc(misc_written, 1)
                elif s[0] == "route":
                    L, b = s[1], s[2]
                    for t in range(NT):
                        ins = pe.matmul(ps_misc[:, t * E:(t + 1) * E], hT[b][:, t * 128:(t + 1) * 128],
                                        cols[:, COL_RW + L * E:COL_RW + (L + 1) * E], start=True, stop=True)
                    ins.then_inc(misc_written, 1)
                elif s[0] == "fc1":
                    L, k = s[1], s[2]
                    e, b = divmod(k, 2)
                    i = (L * E + e) % WSLOT
                    pe.wait_ge(w_split, 2 * (L * E + e + 1))
                    if k < 2:
                        pe.wait_ge(hlo_ready, 2 * L + b + 1)
                    if k == 0:
                        pe.wait_ge(probs_ready, units_before(16 * (L + 1)))
                    for c in range(NC):
                        f = 64 * L + NC * k + c
                        if f >= 4:
                            pe.wait_ge(hidden_ready, f - 3)
                        m = slice(c * 128, (c + 1) * 128)
                        pe.matmul(fc1_bank(f), w_hi[i][:, m], hT_hi[b][:, :], start=True, stop=False)
                        pe.matmul(fc1_bank(f), w_hi[i][:, m], hT_lo[b][:, :], start=False, stop=False)
                        pe.matmul(fc1_bank(f), w_lo[i][:, m], hT_hi[b][:, :], start=False,
                                  stop=True).then_inc(fc1_written, 1)
                elif s[0] == "cbc":
                    L, k = s[1], s[2]
                    e, b = divmod(k, 2)
                    if k < 2:
                        pe.wait_ge(comb_ready, 2 * L + b + 1)
                    if k == 0:
                        pe.wait_ge(o_ready, 16 * (L + 1))
                    if 16 * L + k:
                        pe.wait_ge(gate_ready, 16 * L + k)
                    for t in range(NT):
                        ins = pe.transpose(ps_o[:, t * 128:(t + 1) * 128],
                                           comb[b][:, t, e:e + 1].to_broadcast([128, 128]), ident[:, :])
                    ins.then_inc(gate_written, 1)
                elif s[0] == "fc2":
                    L, k = s[1], s[2]
                    e, b = divmod(k, 2)
                    i = (L * E + e) % WSLOT
                    pe.wait_ge(w_loaded[i], 32 * ((L * E + e) // WSLOT + 1))
                    if k == 0:
                        pe.wait_ge(max_read, maxes_before(16 * (L + 1)))
                    if 16 * L + k >= 2:
                        pe.wait_ge(fc2_read, 16 * L + k - 1)
                    for c in range(NC):
                        pe.wait_ge(hidden_ready, 64 * L + NC * k + c + 1)
                        ins = pe.matmul(ps_max[k % 2][:, :], w2[i][:, c * 128:(c + 1) * 128], hidden(k, c),
                                        start=c == 0, stop=c == NC - 1)
                    ins.then_inc(fc2_written, 1)
                elif s[0] == "mout":
                    L, b = s[1], s[2]
                    pe.wait_ge(acc_added, 14 * L + 13 + b)
                    for t in range(NT):
                        ins = pe.transpose(ps_misc[:, t * 128:(t + 1) * 128], acc[b][:, t * 128:(t + 1) * 128],
                                           ident[:, :])
                    ins.then_inc(misc_written, 1)

        @block.vector
        def _(dve):
            chain = [0]

            def link(ins):
                chain[0] += 1
                ins.then_inc(dve_chain, 1)
                dve.wait_ge(dve_chain, chain[0])

            def tiles(ap):
                return ap.rearrange("p (t d) -> p t d", d=128)

            for t in v_aug:
                dve.memset(t[:, :, :, :], 0.0)
            link(dve.memset(vc_aug[:, :, :, :], 0.0))
            for t in v_aug:
                dve.memset(t[:, :, :, HD:HD + 1], 1.0)
            link(dve.memset(vc_aug[:, :, :, HD:HD + 1], 1.0))
            dve.wait_ge(ident_ready, 1)
            dve.wait_ge(consts_loaded, 16)
            exps = 0
            masks_made = False
            for s in PLAN:
                if s in MISC and s[0] in ("vproj", "cvproj", "mt", "otr", "oproj", "route", "mout") and s[0] != "mt":
                    dve.wait_ge(misc_written, MISC[s] + 1)
                if s[0] == "norm":
                    d = s[1]
                    if d == "ctx":
                        i, p, src, dst = 2, SE, ctx_x, ctx_hat
                        dve.wait_ge(ctx_loaded, 16)
                    else:
                        i, p, src, dst = d % 2, 128, x[d % 2], xhat[d % 2]
                        if d < 2:
                            dve.wait_ge(x_loaded, 16 * B)
                    nt = src.shape[1]
                    for t in range(nt):
                        ins = dve.bn_stats(stats[0:p, i, t, :], src[:, t, :])
                    link(ins)
                    for t in range(nt):
                        ins = dve.bn_aggr(mv[0:p, i, t, :], stats[0:p, i, t, :])
                    ins.then_inc(var_ready, 1)
                    y, sq, out_r = rstd[0:p, i, 1, 0:nt], rstd[0:p, i, 2, 0:nt], rstd[0:p, i, 3, 0:nt]
                    dve.wait_ge(rstd_raw, ORD[s] + 1)
                    link(dve.tensor_tensor(sq, y, y, ALU.mult))
                    link(dve.scalar_tensor_tensor(sq, mv[0:p, i, 0:nt, 1], EPS, sq, ALU.add, ALU.mult))
                    link(dve.tensor_scalar(sq, sq, -0.5, 1.5, ALU.mult, ALU.add))
                    link(dve.tensor_tensor(out_r, y, sq, ALU.mult))
                    for t in range(nt):
                        ins = dve.tensor_scalar(dst[:, t, :], src[:, t, :], mv[0:p, i, t, 0:1],
                                                rstd[0:p, i, 3, t:t + 1], ALU.subtract, ALU.mult)
                    ins.then_inc(xhat_ready, 1)
                elif s[0] == "vproj":
                    n = s[1]
                    dve.wait_ge(rows_ready, 1)
                    if n >= 4:
                        dve.wait_ge(av_done, avs_before(4 * (n - 3)))
                    dve.tensor_tensor(
                        v_aug[n % 2][:, :, :, 0:HD], ps_misc[:, :].rearrange("p (t h d) -> p t h d", t=NT, h=H),
                        row(ROW_BV + att_of(n)).rearrange("p t (h d) -> p t h d", h=H), ALU.add).then_inc(misc_done, 1)
                elif s[0] == "cvproj":
                    L = s[1]
                    dve.wait_ge(rows_ready, 1)
                    if L == 1:
                        dve.wait_ge(av_done, avs_before(16))
                    dve.tensor_tensor(
                        vc_aug[:, :, :, 0:HD],
                        ps_misc[0:SE, 0:B * 128].rearrange("p (t h d) -> p t h d", t=B, h=H),
                        row(ROW_BV + 2 * L + 1, SE, B).rearrange("p t (h d) -> p t h d", h=H),
                        ALU.add).then_inc(misc_done, 1)
                elif s[0] == "max":
                    G, i = s[1], s[2]
                    n = G // NG
                    m = MAX[s]
                    dve.wait_ge(max_written, m + 1)
                    if is_self(n):
                        qb, j = divmod(i, GH)
                        w = (qb + 1) * 128 if causal(n) else S
                        dve.tensor_reduce(m_raw[G % 2][:, qb, j:j + 1], ps_max[m % 2][:, 0:w], AX.X,
                                          ALU.max).then_inc(max_read, 1)
                    else:
                        dve.tensor_reduce(m_raw[G % 2][:, i, :], tiles(ps_max[m % 2][:, :])[:, :, 0:SE], AX.X,
                                          ALU.max).then_inc(max_read, 1)
                elif s[0] == "mt":
                    G = s[1]
                    dve.wait_ge(pads_ready, 1)
                    dve.wait_ge(max_read, maxes_before(G + 1))
                    heads = m_cols[:, :, :].rearrange("p t (j c) -> p t j c", c=32)
                    hi, lo = heads[:, :, :, 24], heads[:, :, :, 25]
                    link(dve.tensor_scalar(hi.bitcast(f32r), m_raw[G % 2][:, :, :], -1.0, None, ALU.mult))
                    dve.scalar_tensor_tensor(lo, m_raw[G % 2][:, :, :], -1.0, hi, ALU.mult,
                                             ALU.subtract).then_inc(mcols_ready, 1)
                    dve.wait_ge(misc_written, MISC[s] + 1)
                    dve.wait_ge(stack_ready, SPLIT[("proj", G, "q")] + 1)
                    if G >= 2:
                        dve.wait_ge(scores_written, units_before(G - 1))
                    dve.tensor_tensor(q_max[G % 2][:, :], ps_misc[:, :], q_st[G % QRING][:, :].bitcast(f32),
                                      ALU.add).then_inc(misc_done, 1)
                    if not masks_made:
                        masks_made = True
                        dve.wait_ge(masks_ready, 1)
                        dve.tensor_copy(ident_r[:, :], ident[:, :])
                        dve.tensor_copy(mask_r[:, :, :], mask[:, :, :]).then_inc(masks_ready, 1)
                elif s[0] == "otr":
                    G = s[1]
                    b, g = G // NG % 2, G % NG
                    o = ps_misc[:, :].rearrange("p (i c) -> p i c", c=32)
                    link(dve.reciprocal(rden[:, :], o[:, :, HD]))
                    dve.tensor_tensor(a_tok[b][:, :, g * 32:(g + 1) * 32].rearrange("p t (j d) -> p t j d", d=HD),
                                      ps_misc[:, :].rearrange("p (t j c) -> p t j c", j=GH, c=32)[:, :, :, 0:HD],
                                      rden[:, :].rearrange("p (t j) -> p t j", j=GH).unsqueeze(3)
                                      .to_broadcast([128, NT, GH, HD]), ALU.mult).then_inc(misc_done, 1)
                elif s[0] == "oproj":
                    n = s[1]
                    b = n % 2
                    dve.wait_ge(res_ready, ORD[("resid", n)] + 1)
                    dve.tensor_tensor(x[b][:, :, :], tiles(ps_misc[:, :]), res[b][:, :, :],
                                      ALU.add).then_inc(misc_done, 1)
                    dve.wait_ge(misc_done, MISC[s] + 1)
                elif s[0] == "route":
                    L, b = s[1], s[2]

                    def top(lg, m, one):
                        link(dve.tensor_reduce(rs[:, m, :], lg, AX.X, ALU.max))
                        link(dve.tensor_tensor(r[:, 3, :, :], lg, over_experts(rs[:, m, :]), ALU.is_equal))
                        link(dve.tensor_tensor(r[:, 3, :, :], r[:, 3, :, :],
                                               over_tiles(cols[:, COL_DESC:COL_DESC + E]), ALU.mult))
                        link(dve.tensor_reduce(rs[:, 0, :], r[:, 3, :, :], AX.X, ALU.max))
                        link(dve.tensor_tensor(one, r[:, 3, :, :], over_experts(rs[:, 0, :]), ALU.is_equal))

                    lg, one1, one2, rest = r[:, 0, :, :], r[:, 4, :, :], r[:, 5, :, :], r[:, 6, :, :]
                    dve.tensor_tensor(lg, ps_misc[:, 0:NT * E].rearrange("p (t e) -> p t e", e=E),
                                      over_tiles(cols[:, COL_RB + L * E:COL_RB + (L + 1) * E]),
                                      ALU.add).then_inc(misc_done, 1)
                    dve.wait_ge(misc_done, MISC[s] + 1)
                    if L == 1:
                        link(dve.tensor_reduce(rs[:, 0, :], lg, AX.X, ALU.max))
                        dve.tensor_tensor(r[:, 1, :, :], lg, over_experts(rs[:, 0, :]),
                                          ALU.subtract).then_inc(exp_in, 1)
                        exps += 1
                        dve.wait_ge(exp_out, exps)
                        link(dve.tensor_reduce(rs[:, 1, :], r[:, 2, :, :], AX.X, ALU.add))
                        link(dve.reciprocal(rs[:, 2, :], rs[:, 1, :]))
                        link(dve.tensor_tensor(lg, r[:, 2, :, :], over_experts(rs[:, 2, :]), ALU.mult))
                    top(lg, 3, one1)
                    link(dve.scalar_tensor_tensor(rest, one1, -BIG, lg, ALU.mult, ALU.add))
                    top(rest, 4, one2)
                    dve.tensor_tensor(rs[:, 7, :], rs[:, 4, :], rs[:, 3, :], ALU.subtract).then_inc(exp_in, 1)
                    exps += 1
                    dve.wait_ge(exp_out, exps)
                    link(dve.tensor_scalar_add(rs[:, 5, :], rs[:, 8, :], 1.0))
                    link(dve.reciprocal(rs[:, 6, :], rs[:, 5, :]))
                    dve.tensor_tensor(one1, one1, over_experts(rs[:, 6, :]), ALU.mult)
                    link(dve.tensor_tensor(rs[:, 5, :], rs[:, 8, :], rs[:, 6, :], ALU.mult))
                    link(dve.tensor_tensor(one2, one2, over_experts(rs[:, 5, :]), ALU.mult))
                    dve.tensor_tensor(comb[b][:, :, :], one1, one2, ALU.add).then_inc(comb_ready, 1)
                elif s[0] == "fc2":
                    L, k = s[1], s[2]
                    e, b = divmod(k, 2)
                    dve.wait_ge(fc2_written, 16 * L + k + 1)
                    dve.wait_ge(gate_ready, 16 * L + k + 1)
                    if k >= 4:
                        dve.wait_ge(acc_added, 14 * L + k - 3)
                    dst = acc[b] if e == 0 else eo[k % 2]
                    dve.scalar_tensor_tensor(dst[:, :], ps_max[k % 2][:, :], col(COL_B2 + L * E + e),
                                             gate_bc[k % 2][:, :], ALU.add, ALU.mult).then_inc(fc2_read, 1)
                elif s[0] == "mout":
                    L, b = s[1], s[2]
                    if L == 1:
                        dve.wait_ge(res_ready, ORD[("resid", MOE + 2 + b)] + 1)
                    dve.tensor_tensor(x[b][:, :, :], tiles(ps_misc[:, :]), (x if L == 0 else res)[b][:, :, :],
                                      ALU.add).then_inc(misc_done, 1)
                    dve.wait_ge(misc_done, MISC[s] + 1)
                elif s[0] == "final":
                    b = s[1]
                    dve.wait_ge(xhat_ready, ORD[("norm", LAST + b)] + 1)
                    link(dve.tensor_tensor(xhat[b][:, :, :], xhat[b][:, :, :], row(ROW_LN + 4), ALU.mult))
                    dve.tensor_tensor(res[b][:, :, :], xhat[b][:, :, :], row(ROW_LN + 5), ALU.add).then_inc(final_ready, 1)


ATTENTIONS = ("L0_xattn_sa", "L0_xattn_ca", "L1_xattn_sa", "L1_xattn_ca")


def attention_weights(inputs, np, a):
    t = ATTENTIONS[a]
    if a < 2:
        w, b = inputs[t + "_in_w"], inputs[t + "_in_b"]
        ws = [w[i * D:(i + 1) * D].T for i in range(3)] + [inputs[t + "_out_w"].T]
        bs = [b[i * D:(i + 1) * D] for i in range(3)] + [inputs[t + "_out_b"]]
    else:
        ws = [inputs[t + "_w" + c] for c in "qkvo"]
        bs = [inputs[t + "_b" + c] for c in "qkvo"]
    return ws, bs


def stack_heads(w, np):
    w = w.reshape(-1, NG, GH, 1, HD)
    return np.concatenate([w, w, w, np.zeros_like(w)], axis=3).reshape(-1, NG, GH * 32)


def kernel(**inputs):
    import numpy as np
    import concourse.bacc as bacc
    from concourse.bass_utils import run_bass_kernel_spmd

    inputs = {k: np.asarray(v) for k, v in inputs.items()}
    f = np.float32
    cols = np.zeros((128, NCOL), f)
    rows = np.zeros((NROW, 128), f)
    watt = np.zeros((4, 128, ATT), f)
    row_of = np.arange(128) % 32
    for a in range(4):
        (wq, wk, wv, wo), (bq, bk, bv, bo) = attention_weights(inputs, np, a)
        watt[a, :, 0:512] = stack_heads(wq, np).reshape(128, 512)
        watt[a, :, 512:1024] = stack_heads(wk, np).reshape(128, 512)
        watt[a, :, 1024:1152], watt[a, :, 1152:1280] = wv, wo
        cols[:, COL_BQ + 4 * a:COL_BQ + 4 * a + 4] = stack_heads(bq[None], np)[0].T
        cols[:, COL_BK + 4 * a:COL_BK + 4 * a + 4] = stack_heads(bk[None], np)[0].T
        rows[ROW_BV + a], rows[ROW_BO + a] = bv, bo
    cols[(row_of == 24) | (row_of == 25), COL_BK:COL_BK + 16] = 1.0
    norms = ("L0_xattn_sa_ln", "L0_xattn_ca_q_ln", "L0_xattn_ca_kv_ln", "L0_xattn_moe_ln", "L1_xattn_ln1", "L1_xattn_ln2")
    for i, t in enumerate(norms):
        cols[:, COL_LN + 2 * i], cols[:, COL_LN + 2 * i + 1] = inputs[t + "_g"], inputs[t + "_b"]
    for i in range(3):
        rows[ROW_LN + 2 * i], rows[ROW_LN + 2 * i + 1] = inputs[f"L1_xattn_ln{i + 1}_g"], inputs[f"L1_xattn_ln{i + 1}_b"]
    q_lo, k_lo = row_of // HD == 2, row_of // HD == 1
    cols[q_lo, COL_QLO], cols[k_lo, COL_KLO] = 1.0, 1.0
    cols[q_lo, COL_BQL:COL_BQL + 16] = cols[q_lo, COL_BQ:COL_BQ + 16]
    cols[k_lo, COL_BKL:COL_BKL + 16] = cols[k_lo, COL_BK:COL_BK + 16]
    cols[:, COL_EPS], cols[:, COL_ONE] = EPS, 1.0
    cols[:, COL_DESC:COL_DESC + E] = np.arange(E, 0, -1)
    w = np.zeros((2 * E, 128, 2 * F), f)
    experts = ((inputs["L0_xattn_e_fc1_w"].transpose(0, 2, 1), inputs["L0_xattn_e_fc2_w"].transpose(0, 2, 1),
                inputs["L0_xattn_e_fc1_b"], inputs["L0_xattn_e_fc2_b"], inputs["L0_xattn_router_w"].T,
                inputs["L0_xattn_router_b"]),
               (inputs["L1_xattn_e_w1"], inputs["L1_xattn_e_w2"], inputs["L1_xattn_e_b1"], inputs["L1_xattn_e_b2"],
                inputs["L1_xattn_router_w"], inputs["L1_xattn_router_b"]))
    for L, (w1, w2, b1, b2, rw, rb) in enumerate(experts):
        w[L * E:(L + 1) * E, :, 0:F] = w1
        w[L * E:(L + 1) * E, :, F:2 * F] = w2.reshape(E, NC, 128, D).transpose(0, 2, 1, 3).reshape(E, 128, F)
        cols[:, COL_B1 + L * E * NC:COL_B1 + (L + 1) * E * NC] = b1.reshape(E * NC, 128).T
        cols[:, COL_B2 + L * E:COL_B2 + (L + 1) * E] = b2.T
        cols[:, COL_RW + L * E:COL_RW + (L + 1) * E] = rw
        cols[:, COL_RB + L * E:COL_RB + (L + 1) * E] = rb[None]
    arrays = {
        "in_x": np.ascontiguousarray(inputs["x"].reshape(B, NT, 128, D).transpose(2, 0, 1, 3)),
        "in_ctx": np.ascontiguousarray(inputs["ctx_1024"].transpose(1, 0, 2)),
        "in_watt": watt, "in_cols": cols, "in_rows": rows, "in_w": w,
    }
    nc = bacc.Bacc("TRN2", target_bir_lowering=False, num_devices=1)
    args = [nc.dram_tensor(name, a.shape, mybir.dt.float32, kind="ExternalInput").ap() for name, a in arrays.items()]
    args.append(nc.dram_tensor("out_0", (128, B, NT, D), mybir.dt.float32, kind="ExternalOutput").ap())
    build(nc, *args)
    got = run_bass_kernel_spmd(nc, [arrays], core_ids=[0]).results[0]["out_0"]
    return np.ascontiguousarray(np.asarray(got).transpose(1, 2, 0, 3)).reshape(B, S, D)
```

```python
import concourse.bass as bass
from concourse import mybir
from contextlib import ExitStack

B, S, D, H, HD, E, F, SE = 2, 512, 128, 16, 8, 8, 512, 77
NT = S // 128
SP = SE + 1
GH = 4
NG = H // GH
NC = F // 128
EPS = 1e-5
BIG = 1e30
ATT = 2 * NG * 128 + 2 * 128
COL_BQ, COL_BK = 0, 16
COL_LN = 32
COL_B1 = 44
COL_B2 = COL_B1 + 2 * E * NC
COL_QLO, COL_KLO = COL_B2 + 2 * E, COL_B2 + 2 * E + 1
COL_BQL = COL_KLO + 1
COL_BKL = COL_BQL + 16
COL_EPS = COL_BKL + 16
COL_ONE = COL_EPS + 1
COL_RW = COL_ONE + 1
COL_RB = COL_RW + 2 * E
COL_DESC = COL_RB + 2 * E
NCOL = COL_DESC + E
LN_SA, LN_CAQ, LN_CTX, LN_MOE, LN_1, LN_2 = range(6)
ROW_BV, ROW_BO, ROW_LN = 0, 4, 8
NROW = 14
KRING, QRING, PRING = 3, 3, 6
HALF_MAGIC, NEWTON = 0x5F3759DF, 4
WSLOT = 4


def causal(n):
    return n in (4, 5)


def is_self(n):
    return n % 4 < 2


def att_of(n):
    return n // 2


MOE, LAST = 10, 20


def goal(n):
    return n + 2 if is_self(n) else MOE + 2 * (n // 4) + n % 2


def n_units(n):
    return 2 * NT if is_self(n) else 2


def n_max(n):
    return GH * NT if is_self(n) else NT


PAIRS = [(0, 0), (1, 0), (2, 0), (0, 1), (1, 1), (2, 1), (3, 0), (3, 1), (4, 0), (4, 1),
         (5, 0), (6, 0), (7, 0), (5, 1), (6, 1), (7, 1)]
LAYER_KEY = 25.5


def make_plan():
    timed = []

    def at(key, *step):
        timed.append((key, len(timed), step))

    for L in range(2):
        t0 = LAYER_KEY * L
        ready = {}
        for b in range(B):
            n = 4 * L + b
            if L == 0:
                at(-9 + b * 0.2, "norm", n)
                ready[n] = -8.5 + b * 0.2
            else:
                ready[n] = t0 - 2.4 if b == 0 else t0 - 0.8
            at(ready[n], "turn", n)
            at(ready[n] + 0.01, "resid", n)
        if L == 0:
            at(-8, "norm", "ctx")
            for e in range(WSLOT):
                at(-7, "wload", 0, e)
        for e in range(WSLOT):
            at(t0 + 0.5 + e, "wsplit", L, e)
        at(t0 + 0.6, "cturn", L)
        at(t0 + 1.3, "cvproj", L)
        for g in range(NG):
            at(t0 + 1.06 + 0.5 * g, "cproj", L, g)
        for n in range(4 * L, 4 * L + 4):
            own = is_self(n)
            if own:
                at(max(t0 - 1.3, t0 + 4 * (n % 4) - 0.8), "vproj", n)
            for g in range(NG):
                G = 4 * n + g
                t = t0 + G - 16 * L
                U, M = n_units(n), n_max(n)
                if own:
                    if n % 4 == 0:
                        at(max(t - 3.1, ready[n] + 0.1 + 0.25 * g), "proj", G, "k")
                        at(max(t - 2.8, ready[n] + 0.2 + 0.25 * g), "proj", G, "q")
                    else:
                        at(max(t - 3.1, ready[n] + 0.05), "proj", G, "k")
                        at(max(t - 2.7, ready[n] + 0.1), "proj", G, "q")
                    lead, spread, lag = 1.5, 1.0, 0.19
                else:
                    q_at = max(t - 3.3, ready[n] + 0.1 + 0.2 * g)
                    at(q_at, "proj", G, "q")
                    lead, spread, lag = min(2.1, t - q_at - 0.3), 0.9, 0.6
                for i in range(M):
                    at(t - lead + spread * i / M, "max", G, i)
                at(t - lead + spread + 0.02, "mcols", G)
                at(t - lead + spread + (0.2 if own else 0.4), "mt", G)
                for u in range(U):
                    at(t + u / U, "unit", G, u)
                for kb in range(U // 2):
                    at(t + (2 * kb + 1) / U + lag, "av", G, kb)
                t += (U - 1) / U + lag
                at(t + 0.01, "oev", G)
                at(t + (0.15 if own else 0.4), "otr", G)
            d = goal(n)
            step = 0.35 if n % 4 in (1, 2) else 0.14
            t = max(t, t + (0.15 if own else 0.4) + 0.12 - step) + step
            for i, k in enumerate(("aturn", "oproj", "norm", "turn", "resid")):
                t += step
                at(t, k, *((d,) if i > 1 else (n,)))
                if k == "oproj" and L == 0 and n % 2:
                    at(t, "watt", 2 + n // 2)
                if k == "turn":
                    ready[d] = t
        for b in range(B):
            at(ready[MOE + 2 * L + b] + 0.2, "route", L, b)
        for i, (e, b) in enumerate(PAIRS):
            t = max(t0 + 16.65, ready[MOE + 2 * L] + 0.25) + 0.5 * i
            at(t - 0.5 + 0.03, "fc1", L, i)
            at(t, "cbc", L, i)
            at(t + 0.04, "fc2", L, i)
            if i == PAIRS.index((E - 1, b)):
                at(t + 0.3 if b == 0 else t + 0.1, "mout", L, b)
            if (e, b) in ((0, 1), (1, 1), (2, 1), (3, 1), (4, 1), (5, 1), (6, 1), (7, 1)):
                nL, ne = divmod(L * E + e + WSLOT, E)
                if nL < 2:
                    at(t + 0.05, "wload", nL, ne)
                    if nL == L:
                        at(t + 0.06, "wsplit", nL, ne)
        if L == 1:
            for b in range(B):
                t = max(k for k, _, s in timed if s == ("mout", 1, b))
                at(t + 0.01, "norm", LAST + b)
                at(t + 0.02, "final", b)
    timed = [(k, o, s) for k, o, s in timed if s not in (("resid", MOE), ("resid", MOE + 1))]
    return [s for _, _, s in sorted(timed)]


PLAN = make_plan()
ORD, _seen = {}, {}
for _s in PLAN:
    ORD[_s] = _seen.get(_s[0], 0)
    _seen[_s[0]] = ORD[_s] + 1
RINGED = ("proj", "cproj", "vproj", "cvproj", "mt", "otr", "aturn", "oproj", "turn", "cturn", "route", "mout",
          "max", "fc2")
RING = {s: i for i, s in enumerate(s for s in PLAN if s[0] in RINGED)}
BANKS = 3
SPLIT = {s: i for i, s in enumerate(s for s in PLAN if s[0] in ("proj", "cproj"))}
KOUT = [s for s in SPLIT if s[0] == "cproj" or s[2] == "k"]
ADDS = {(L, i): 14 * L + sum(1 for e, b in PAIRS[:i] if e) for L in range(2) for i in range(len(PAIRS))}
SELFG = [G for G in range(32) if is_self(G // NG)]


def build(nc, x_in, ctx_in, watt_in, cols_in, rows_in, w_in, out):
    f32, f32r, i32 = mybir.dt.float32, mybir.dt.float32r, mybir.dt.int32
    ALU = mybir.AluOpType
    ACT = mybir.ActivationFunctionType
    AX = mybir.AxisListType

    ctx = ExitStack()
    with ctx:
        def sb(name, shape, dt=f32):
            return ctx.enter_context(nc.sbuf_tensor(name, shape, dt))

        def sem(name):
            return ctx.enter_context(nc.semaphore(name))

        ident = sb("ident", [128, 128])
        ident_r = sb("ident_r", [128, 128], f32r)
        mask = sb("mask", [128, 2, 128])
        mask_r = sb("mask_r", [128, 2, 128], f32r)
        cols = sb("cols", [128, NCOL])
        rows = sb("rows", [128, NROW, 128])
        watt = [sb(f"watt{i}", [128, ATT]) for i in range(2)]
        x = [sb(f"x{b}", [128, NT, 128]) for b in range(B)]
        res = [sb(f"res{b}", [128, NT, 128]) for b in range(B)]
        xhat = [sb(f"xhat{b}", [128, NT, 128]) for b in range(B)]
        hT = [sb(f"hT{b}", [128, S]) for b in range(B)]
        hT_hi = [sb(f"hT_hi{b}", [128, S], f32r) for b in range(B)]
        hT_lo = [sb(f"hT_lo{b}", [128, S], f32r) for b in range(B)]
        ctx_x = sb("ctx_x", [SE, B, 128])
        ctx_hat = sb("ctx_hat", [SE, B, 128])
        ctxT = sb("ctxT", [128, B, SP])
        stats = sb("stats", [128, 3, NT, 6])
        mv = sb("mv", [128, 3, NT, 2])
        rstd = sb("rstd", [128, 3, 4, NT])
        split_y = [sb(f"split_y{i}", [128, S]) for i in range(2)]
        split_hi = [sb(f"split_hi{i}", [128, S], f32r) for i in range(2)]
        k_out = [sb(f"k_out{i}", [128, S], f32r) for i in range(2)]
        q_st = [sb(f"q_st{i}", [128, S], f32r) for i in range(QRING)]
        q_max = [sb(f"q_max{i}", [128, S], f32r) for i in range(2)]
        k_m = [sb(f"k_m{i}", [128, GH, S], f32r) for i in range(KRING)]
        kc_m = sb("kc_m", [128, NG, GH, B * SP], f32r)
        v_aug = [sb(f"v_aug{i}", [128, NT, H, 32]) for i in range(2)]
        vc_aug = sb("vc_aug", [SE, B, H, 32])
        m_raw = [sb(f"m_raw{i}", [128, NT, GH]) for i in range(2)]
        m_cols = sb("m_cols", [128, NT, 128])
        P = [sb(f"P{i}", [128, 2, S]) for i in range(PRING)]
        o_sb = [sb(f"o_sb{i}", [128, S]) for i in range(2)]
        rden = [sb(f"rden{i}", [128, NT * GH]) for i in range(2)]
        a_tok = [sb(f"a_tok{b}", [128, NT, 128]) for b in range(B)]
        aT = sb("aT", [128, S])
        w_hi = [sb(f"w_hi{i}", [128, F], f32r) for i in range(WSLOT)]
        w_lo = [sb(f"w_lo{i}", [128, F], f32r) for i in range(WSLOT)]
        w2 = [sb(f"w2{i}", [128, NC * 128]) for i in range(WSLOT)]
        w_raw = [sb(f"w_raw{i}", [128, F]) for i in range(WSLOT)]
        r = sb("r", [128, 7, NT, E])
        rs = sb("rs", [128, 9, NT])
        comb = [sb(f"comb{b}", [128, NT, E]) for b in range(B)]
        gate_bc = [sb(f"gate_bc{i}", [128, S]) for i in range(2)]
        eo = [sb(f"eo{i}", [128, S]) for i in range(2)]
        acc = [sb(f"acc{b}", [128, S]) for b in range(B)]

        ps = [ctx.enter_context(nc.psum_tensor(f"ps_ring{i}", [128, S], f32)) for i in range(BANKS)]
        ps_sc = [ctx.enter_context(nc.psum_tensor(f"ps_sc{i}", [128, 2, S], f32)) for i in range(2)]
        ps_o = ctx.enter_context(nc.psum_tensor("ps_o", [128, S], f32))

        written = [sem(f"bank_written{i}") for i in range(BANKS)]
        done = [sem(f"bank_done{i}") for i in range(BANKS)]
        consts_loaded, x_loaded, ctx_loaded = sem("consts_loaded"), sem("x_loaded"), sem("ctx_loaded")
        rows_loaded = sem("rows_loaded")
        watt_loaded = [sem("watt_loaded0"), sem("watt_loaded1")]
        ident_ready, masks_ready, pads_ready = sem("ident_ready"), sem("masks_ready"), sem("pads_ready")
        vpads_ready, rows_ready = sem("vpads_ready"), sem("rows_ready")
        xhat_ready = sem("xhat_ready")
        stack_ready, hlo_ready, res_ready = sem("stack_ready"), sem("hlo_ready"), sem("res_ready")
        k_moved = [sem(f"k_moved{i}") for i in range(KRING)]
        kc_moved = [sem(f"kc_moved{i}") for i in range(2)]
        mcols_ready = sem("mcols_ready")
        scores_written, probs_ready, av_done = sem("scores_written"), sem("probs_ready"), sem("av_done")
        o_ready = sem("o_ready")
        w_loaded = [sem(f"w_loaded{i}") for i in range(WSLOT)]
        w_split = sem("w_split")
        exp_in, exp_out, comb_ready = sem("exp_in"), sem("exp_out"), sem("comb_ready")
        fc1_written, hidden_ready = sem("fc1_written"), sem("hidden_ready")
        gate_written, gate_ready, acc_added = sem("gate_written"), sem("gate_ready"), sem("acc_added")
        final_ready, stored = sem("final_ready"), sem("stored")
        dve_chain, act_chain, pool_chain = sem("dve_chain"), sem("act_chain"), sem("pool_chain")

        def col(i, p=128):
            return cols[0:p, i:i + 1]

        def row(i, p=128, n=NT):
            return rows[0:p, i, :].unsqueeze(1).to_broadcast([p, n, 128])

        def over_tiles(ap):
            return ap.unsqueeze(1).to_broadcast([128, NT, E])

        def over_experts(ap):
            return ap.unsqueeze(2).to_broadcast([128, NT, E])

        def bank_of(step):
            return ps[RING[step] % BANKS]

        def wait_written(eng, step):
            eng.wait_ge(written[RING[step] % BANKS], RING[step] // BANKS + 1)

        def wait_done(eng, step):
            eng.wait_ge(done[RING[step] % BANKS], RING[step] // BANKS + 1)

        def kslot(G):
            return SELFG.index(G) % KRING

        def kuse(G):
            return SELFG.index(G) // KRING + 1

        def kc_count(k):
            return sum(1 for i in range(k % 2, k + 1, 2) if KOUT[i][0] == "cproj")

        def avs_before(G):
            return sum(n_units(g // NG) // 2 for g in range(G))

        def units_before(G):
            return sum(n_units(g // NG) for g in range(G))

        def maxes_before(G):
            return sum(n_max(g // NG) for g in range(G))

        UNIT_GROUP = [(G, u) for G in range(32) for u in range(n_units(G // NG))]

        def hidden(k, c):
            return P[(2 * k) % PRING + c // 2][:, c % 2, :]

        def fc1_bank(f):
            return ps_sc[f % 4 // 2][:, f % 2, :]

        def q0_of(G, kb):
            return kb * 128 if causal(G // NG) else 0

        block = ctx.enter_context(nc.Block())

        @block.sync
        def _(sp):
            sp.dma_start(x[0][:, :, :], x_in[:, 0, :, :]).then_inc(x_loaded, 16)
            sp.dma_start(cols[:, :], cols_in).then_inc(consts_loaded, 16)
            sp.dma_start(watt[0][:, :], watt_in[0]).then_inc(watt_loaded[0], 16)
            sp.dma_start(x[1][:, :, :], x_in[:, 1, :, :]).then_inc(x_loaded, 16)
            sp.dma_start(ctx_x[:, :, :], ctx_in).then_inc(ctx_loaded, 16)
            sp.dma_start(rows[:, :, :], rows_in.unsqueeze(0).to_broadcast([128, NROW, 128])).then_inc(rows_loaded, 16)
            sp.dma_start(watt[1][:, :], watt_in[1]).then_inc(watt_loaded[1], 16)
            sp.wait_ge(pads_ready, 1)
            for s in PLAN:
                if s[0] == "watt":
                    a = s[1]
                    wait_written(sp, ("oproj", 2 * (a - 2) + 1))
                    sp.dma_start(watt[a % 2][:, :], watt_in[a]).then_inc(watt_loaded[a % 2], 16)
                elif s[0] == "proj" and s[2] == "k":
                    G = s[1]
                    sp.wait_ge(stack_ready, SPLIT[s] + 1)
                    if kuse(G) > 1:
                        sp.wait_ge(scores_written, units_before(SELFG[SELFG.index(G) - KRING] + 1))
                    for j in range(GH):
                        p = slice(32 * j, 32 * j + 32)
                        sp.dma_start(k_m[kslot(G)][p, j, :].bitcast(f32),
                                     k_out[KOUT.index(s) % 2][p, :].bitcast(f32)).then_inc(k_moved[kslot(G)], 16)
                elif s[0] == "cproj":
                    L, g = s[1], s[2]
                    sp.wait_ge(stack_ready, SPLIT[s] + 1)
                    if L == 1:
                        sp.wait_ge(scores_written, units_before(16))
                    for j in range(GH):
                        p = slice(32 * j, 32 * j + 32)
                        sp.dma_start(kc_m[p, g, j, :].bitcast(f32),
                                     k_out[KOUT.index(s) % 2][p, 0:B * SP].bitcast(f32)).then_inc(kc_moved[KOUT.index(s) % 2], 16)
                elif s[0] == "wload":
                    L, e = s[1], s[2]
                    k = L * E + e
                    if k >= WSLOT:
                        L0, e0 = divmod(k - WSLOT, E)
                        wait_written(sp, ("fc2", L0, PAIRS.index((e0, 1))))
                        sp.wait_ge(w_split, 2 * (k - WSLOT + 1))
                    sp.dma_start(w_raw[k % WSLOT][:, :], w_in[k, :, 0:F]).then_inc(w_loaded[k % WSLOT], 16)
                    sp.dma_start(w2[k % WSLOT][:, :], w_in[k, :, F:2 * F]).then_inc(w_loaded[k % WSLOT], 16)
                elif s[0] == "final":
                    b = s[1]
                    sp.wait_ge(final_ready, b + 1)
                    sp.dma_start(out[:, b, :, :], res[b][:, :, :]).then_inc(stored, 16)
            sp.wait_ge(stored, 16 * B)

        @block.gpsimd
        def _(pool):
            chain = [0]

            def link(ins):
                chain[0] += 1
                ins.then_inc(pool_chain, 1)
                pool.wait_ge(pool_chain, chain[0])

            link(pool.memset(ident[:, :], 0.0))
            pool.affine_select(out=ident[:, :], in_=ident[:, :], compare_op=ALU.not_equal, fill=1.0, base=0,
                               pattern=[[-1, 128]], channel_multiplier=1).then_inc(ident_ready, 1)
            pool.memset(ctxT[:, :, :], 0.0)
            for t in k_m:
                pool.memset(t[:, :, :].bitcast(f32), 0.0)
            pool.memset(kc_m[:, :, :, :].bitcast(f32), 0.0)
            pool.memset(m_cols[:, :, :], 0.0).then_inc(pads_ready, 1)
            link(pool.memset(mask[:, :, :], 0.0))
            pool.affine_select(out=mask[:, 0, :], in_=mask[:, 0, :], compare_op=ALU.is_ge, fill=-BIG, base=0,
                               pattern=[[-1, 128]], channel_multiplier=1)
            pool.affine_select(out=mask[:, 1, :], in_=mask[:, 1, :], compare_op=ALU.is_ge, fill=-BIG, base=0,
                               pattern=[[1, 128]], channel_multiplier=-1).then_inc(masks_ready, 1)
            pool.wait_ge(consts_loaded, 16)
            pool.wait_ge(rows_loaded, 16)
            pool.tensor_tensor(rows[:, ROW_LN + 1, :], rows[:, ROW_LN + 1, :], rows[:, ROW_BO + 3, :],
                               ALU.add).then_inc(rows_ready, 1)
            pool.wait_ge(rows_ready, 1)
            for s in PLAN:
                if s in SPLIT:
                    i = SPLIT[s]
                    w = S if s[0] == "proj" else B * SP
                    wait_done(pool, s)
                    if s[0] == "proj" and s[2] == "q":
                        G = s[1]
                        if G >= QRING:
                            wait_done(pool, ("mt", G - QRING))
                        dst = q_st[G % QRING]
                    else:
                        k = KOUT.index(s)
                        if k >= 2:
                            t = KOUT[k - 2]
                            if t[0] == "cproj":
                                pool.wait_ge(kc_moved[k % 2], 64 * kc_count(k - 2))
                            else:
                                pool.wait_ge(k_moved[kslot(t[1])], 64 * kuse(t[1]))
                        dst = k_out[k % 2]
                    pool.tensor_tensor(dst[:, 0:w], split_y[i % 2][:, 0:w], split_hi[i % 2][:, 0:w].bitcast(f32),
                                       ALU.subtract).then_inc(stack_ready, 1)
                elif s[0] == "resid":
                    d = s[1]
                    b = d % 2
                    if d < 6:
                        if d < 2:
                            pool.wait_ge(x_loaded, 16 * B)
                        else:
                            wait_done(pool, ("oproj", d - 2) if d < 4 else ("mout", 0, b))
                        pool.tensor_tensor(res[b][:, :, :], x[b][:, :, :], row(ROW_BO + d // 2),
                                           ALU.add).then_inc(res_ready, 1)
                    elif d in (6, 7, MOE + 2, MOE + 3):
                        r0 = ROW_LN + (0 if d < MOE else 2)
                        pool.wait_ge(xhat_ready, ORD[("norm", d)] + 1)
                        link(pool.tensor_tensor(res[b][:, :, :], xhat[b][:, :, :], row(r0), ALU.mult))
                        pool.tensor_tensor(res[b][:, :, :], res[b][:, :, :], row(r0 + 1),
                                           ALU.add).then_inc(res_ready, 1)
                elif s[0] == "turn" and s[1] >= MOE:
                    b = s[1] % 2
                    wait_done(pool, s)
                    pool.tensor_tensor(hT_lo[b][:, :], hT[b][:, :], hT_hi[b][:, :].bitcast(f32),
                                       ALU.subtract).then_inc(hlo_ready, 1)
                elif s[0] == "wsplit":
                    k = s[1] * E + s[2]
                    i = k % WSLOT
                    pool.wait_ge(w_loaded[i], 32 * (k // WSLOT + 1))
                    pool.tensor_copy(w_hi[i][:, :], w_raw[i][:, :]).then_inc(w_split, 1)
                    pool.wait_ge(w_split, 2 * k + 1)
                    pool.tensor_tensor(w_lo[i][:, :], w_raw[i][:, :], w_hi[i][:, :].bitcast(f32),
                                       ALU.subtract).then_inc(w_split, 1)
                elif s[0] == "fc2" and PAIRS[s[2]][0]:
                    L, i = s[1], s[2]
                    b = PAIRS[i][1]
                    wait_done(pool, s)
                    if ADDS[L, i]:
                        pool.wait_ge(acc_added, ADDS[L, i])
                    pool.tensor_tensor(acc[b][:, :], acc[b][:, :], eo[i % 2][:, :], ALU.add).then_inc(acc_added, 1)

        @block.scalar
        def _(act):
            chain = [0]

            def link(ins):
                chain[0] += 1
                ins.then_inc(act_chain, 1)
                act.wait_ge(act_chain, chain[0])

            exps = 0
            act.wait_ge(consts_loaded, 16)
            for s in PLAN:
                if s[0] in ("proj", "cproj", "turn", "cturn", "aturn"):
                    wait_written(act, s)
                    bank = bank_of(s)
                if s in SPLIT:
                    i = SPLIT[s]
                    n = s[1] // NG if s[0] == "proj" else 4 * s[1] + 2
                    g = s[1] % NG if s[0] == "proj" else s[2]
                    w = S if s[0] == "proj" else B * SP
                    a = 4 * (n // 2) + g
                    bias, bias_lo, lo = ((col(COL_BQ + a), col(COL_BQL + a), col(COL_QLO)) if s[-1] == "q" else
                                         (col(COL_BK + a), col(COL_BKL + a), col(COL_KLO)))
                    if i >= 2:
                        act.wait_ge(stack_ready, i - 1)
                    act.activation(split_y[i % 2][:, 0:w], bank[:, 0:w], ACT.Identity, bias=bias)
                    act.activation(split_hi[i % 2][:, 0:w], bank[:, 0:w], ACT.Identity,
                                   bias=bias_lo, scale=lo).then_inc(done[RING[s] % BANKS], 1)
                elif s[0] == "turn":
                    d = s[1]
                    b = d % 2
                    if d in (4, 5):
                        gain, shift = 1.0, 0.0
                    else:
                        ln = {0: LN_SA, 1: LN_CAQ, 3: LN_1, 5: LN_MOE, 6: LN_2}[d // 2]
                        gain, shift = col(COL_LN + 2 * ln), col(COL_LN + 2 * ln + 1)
                    if d >= MOE:
                        act.activation(hT_hi[b][:, :], bank[:, :], ACT.Identity, bias=shift, scale=gain)
                    act.activation(hT[b][:, :], bank[:, :], ACT.Identity, bias=shift,
                                   scale=gain).then_inc(done[RING[s] % BANKS], 1)
                elif s[0] == "cturn":
                    gain, shift = (col(COL_LN + 2 * LN_CTX), col(COL_LN + 2 * LN_CTX + 1)) if s[1] == 0 else (1.0, 0.0)
                    act.wait_ge(pads_ready, 1)
                    act.activation(ctxT[:, :, 0:SE], bank[:, 0:B * SP].rearrange("p (b s) -> p b s", b=B)[:, :, 0:SE],
                                   ACT.Identity, bias=shift, scale=gain).then_inc(done[RING[s] % BANKS], 1)
                elif s[0] == "aturn":
                    act.activation(aT[:, :], bank[:, :], ACT.Identity).then_inc(done[RING[s] % BANKS], 1)
                elif s[0] == "unit":
                    G, u = s[1], s[2]
                    t = units_before(G) + u
                    kb = u // 2
                    p = 128 if is_self(G // NG) else SE
                    w = S - q0_of(G, kb)
                    act.wait_ge(scores_written, t + 1)
                    if t - PRING >= units_before(16 * (G // 16)):
                        G2, u2 = UNIT_GROUP[t - PRING]
                        act.wait_ge(av_done, avs_before(G2) + u2 // 2 + 1)
                    elif G >= 16:
                        wait_written(act, ("fc2", 0, len(PAIRS) - 1))
                    act.activation(P[t % PRING][0:p, :, 0:w], ps_sc[t % 2][0:p, :, 0:w], ACT.Exp,
                                   scale=float(HD) ** -0.5).then_inc(probs_ready, 1)
                elif s[0] == "oev":
                    G = s[1]
                    act.wait_ge(av_done, avs_before(G + 1))
                    if G >= 2:
                        wait_written(act, ("otr", G - 2))
                    act.activation(o_sb[G % 2][:, :], ps_o[:, :], ACT.Identity).then_inc(o_ready, 1)
                elif s[0] == "route":
                    for n in range(1 + s[1]):
                        exps += 1
                        act.wait_ge(exp_in, exps)
                        src, dst = (r[:, 1, :, :], r[:, 2, :, :]) if s[1] - n == 1 else (rs[:, 7, :], rs[:, 8, :])
                        act.activation(dst, src, ACT.Exp).then_inc(exp_out, 1)
                elif s[0] == "fc1":
                    L, k = s[1], s[2]
                    e = PAIRS[k][0]
                    if k < 3:
                        act.wait_ge(av_done, avs_before(16 * (L + 1)))
                    else:
                        wait_written(act, ("fc2", L, k - 3))
                    for c in range(NC):
                        f = 64 * L + NC * k + c
                        act.wait_ge(fc1_written, f + 1)
                        act.activation(hidden(k, c), fc1_bank(f), ACT.Gelu,
                                       bias=col(COL_B1 + (L * E + e) * NC + c)).then_inc(hidden_ready, 1)
                elif s[0] == "cbc":
                    L, k = s[1], s[2]
                    act.wait_ge(gate_written, 16 * L + k + 1)
                    if k >= 2:
                        wait_done(act, ("fc2", L, k - 2))
                    act.activation(gate_bc[k % 2][:, :], ps_o[:, :], ACT.Identity).then_inc(gate_ready, 1)

        @block.tensor
        def _(pe):
            def turn_tiles(src, bank):
                for t in range(NT):
                    ins = pe.transpose(bank[:, t * 128:(t + 1) * 128], src[:, t, :], ident[:, :])
                return ins

            def wait_attention_weights(a):
                pe.wait_ge(watt_loaded[a % 2], 16 * (a // 2 + 1))

            pe.wait_ge(consts_loaded, 16)
            pe.wait_ge(ident_ready, 1)
            for s in PLAN:
                if s in RING:
                    bank = bank_of(s)
                    if RING[s] >= BANKS:
                        pe.wait_ge(done[RING[s] % BANKS], RING[s] // BANKS)
                if s[0] == "turn":
                    d = s[1]
                    b = d % 2
                    if d in (4, 5):
                        wait_done(pe, ("mout", 0, b))
                        turn_tiles(x[b], bank).then_inc(written[RING[s] % BANKS], 1)
                    else:
                        pe.wait_ge(xhat_ready, ORD[("norm", d)] + 1)
                        turn_tiles(xhat[b], bank).then_inc(written[RING[s] % BANKS], 1)
                elif s[0] == "cturn":
                    src = ctx_hat if s[1] == 0 else ctx_x
                    if s[1] == 0:
                        pe.wait_ge(xhat_ready, ORD[("norm", "ctx")] + 1)
                    for b in range(B):
                        ins = pe.transpose(bank[:, b * SP:b * SP + SE], src[:, b, :], ident[0:SE, 0:SE])
                    ins.then_inc(written[RING[s] % BANKS], 1)
                elif s[0] == "proj":
                    G = s[1]
                    n, g = divmod(G, NG)
                    wait_attention_weights(att_of(n))
                    wait_done(pe, ("turn", n))
                    c = g * 128 + (0 if s[2] == "q" else NG * 128)
                    pe.matmul(bank[:, :], watt[att_of(n) % 2][:, c:c + 128], hT[n % 2][:, :],
                              start=True, stop=True).then_inc(written[RING[s] % BANKS], 1)
                elif s[0] == "cproj":
                    L, g = s[1], s[2]
                    wait_attention_weights(2 * L + 1)
                    wait_done(pe, ("cturn", L))
                    c = (NG + g) * 128
                    pe.matmul(bank[:, 0:B * SP], watt[1][:, c:c + 128], ctxT[:, :, :],
                              start=True, stop=True).then_inc(written[RING[s] % BANKS], 1)
                elif s[0] == "vproj":
                    n = s[1]
                    wait_done(pe, ("turn", n))
                    for t in range(NT):
                        ins = pe.matmul(bank[:, t * 128:(t + 1) * 128], hT[n % 2][:, t * 128:(t + 1) * 128],
                                        watt[att_of(n) % 2][:, 1024:1152], start=True, stop=True)
                    ins.then_inc(written[RING[s] % BANKS], 1)
                elif s[0] == "cvproj":
                    wait_done(pe, ("cturn", s[1]))
                    wait_attention_weights(2 * s[1] + 1)
                    for b in range(B):
                        ins = pe.matmul(bank[0:SE, b * 128:(b + 1) * 128], ctxT[:, b, 0:SE],
                                        watt[1][:, 1024:1152], start=True, stop=True)
                    ins.then_inc(written[RING[s] % BANKS], 1)
                elif s[0] == "max":
                    G, i = s[1], s[2]
                    n, g = divmod(G, NG)
                    if i == 0:
                        pe.wait_ge(stack_ready, SPLIT[("proj", G, "q")] + 1)
                        if is_self(n):
                            pe.wait_ge(k_moved[kslot(G)], 64 * kuse(G))
                        else:
                            for k in [KOUT.index(("cproj", n // 4, c)) for c in range(NG)]:
                                pe.wait_ge(kc_moved[k % 2], 64 * kc_count(k))
                        if n >= 4:
                            pe.wait_ge(masks_ready, 2)
                    dst = bank
                    if is_self(n):
                        qb, j = divmod(i, GH)
                        q = q_st[G % QRING][:, qb * 128:(qb + 1) * 128]
                        w = (qb + 1) * 128 if causal(n) else S
                        ins = pe.matmul(dst[:, 0:w], q, k_m[kslot(G)][:, j, 0:w], start=True, stop=not causal(n))
                        if causal(n):
                            ins = pe.matmul(dst[:, w - 128:w], ident_r[:, :], mask_r[:, 0, :], start=False, stop=True)
                    else:
                        q = q_st[G % QRING][:, i * 128:(i + 1) * 128]
                        for j in range(GH):
                            ins = pe.matmul(dst[:, j * 128:j * 128 + SP], q,
                                            kc_m[:, g, j, (n % 2) * SP:(n % 2 + 1) * SP], start=True, stop=True)
                    ins.then_inc(written[RING[s] % BANKS], 1)
                elif s[0] == "mt":
                    pe.wait_ge(mcols_ready, s[1] + 1)
                    turn_tiles(m_cols, bank).then_inc(written[RING[s] % BANKS], 1)
                elif s[0] == "unit":
                    G, u = s[1], s[2]
                    n, g = divmod(G, NG)
                    t = units_before(G) + u
                    kb, pair = divmod(u, 2)
                    q0 = q0_of(G, kb)
                    if u == 0:
                        wait_done(pe, ("mt", G))
                    if t >= 2:
                        pe.wait_ge(probs_ready, t - 1)
                    if t == units_before(16):
                        pe.wait_ge(hidden_ready, 64)
                    for jj in range(2):
                        j = 2 * pair + jj
                        if is_self(n):
                            dst, k = ps_sc[t % 2][:, jj, 0:S - q0], k_m[kslot(G)][:, j, kb * 128:(kb + 1) * 128]
                        else:
                            dst = ps_sc[t % 2][0:SE, jj, :]
                            k = kc_m[:, g, j, (n % 2) * SP:(n % 2) * SP + SE]
                        ins = pe.matmul(dst, k, q_max[G % 2][:, q0:S], start=True, stop=not causal(n))
                        if causal(n):
                            ins = pe.matmul(ps_sc[t % 2][:, jj, 0:128], ident_r[:, :], mask_r[:, 1, :],
                                            start=False, stop=True)
                    ins.then_inc(scores_written, 1)
                elif s[0] == "av":
                    G, kb = s[1], s[2]
                    n, g = divmod(G, NG)
                    q0 = q0_of(G, kb)
                    w = S - q0
                    if kb == 0:
                        v = ("vproj", n) if is_self(n) else ("cvproj", n // 4)
                        wait_done(pe, v)
                        if G:
                            pe.wait_ge(o_ready, G)
                        if G == 16:
                            pe.wait_ge(gate_ready, 16)
                    t = units_before(G) + 2 * kb
                    pe.wait_ge(probs_ready, t + 2)
                    last = kb == n_units(n) // 2 - 1
                    for j in range(GH):
                        h = GH * g + j
                        if is_self(n):
                            v, pr = v_aug[n % 2][:, kb, h, :], P[(t + j // 2) % PRING][:, j % 2, 0:w]
                        else:
                            v, pr = vc_aug[:, n % 2, h, :], P[(t + j // 2) % PRING][0:SE, j % 2, :]
                        ins = pe.matmul(ps_o[32 * j:32 * j + 32, q0:S], v, pr, start=kb == 0, stop=last)
                    ins.then_inc(av_done, 1)
                elif s[0] == "otr":
                    G = s[1]
                    pe.wait_ge(o_ready, G + 1)
                    for t in range(NT):
                        ins = pe.transpose(bank[:, t * 128:(t + 1) * 128], o_sb[G % 2][:, t * 128:(t + 1) * 128],
                                           ident[:, :])
                    ins.then_inc(written[RING[s] % BANKS], 1)
                elif s[0] == "aturn":
                    for G in range(NG * s[1], NG * (s[1] + 1)):
                        wait_done(pe, ("otr", G))
                    turn_tiles(a_tok[s[1] % 2], bank).then_inc(written[RING[s] % BANKS], 1)
                elif s[0] == "oproj":
                    n = s[1]
                    wait_done(pe, ("aturn", n))
                    for t in range(NT):
                        ins = pe.matmul(bank[:, t * 128:(t + 1) * 128], aT[:, t * 128:(t + 1) * 128],
                                        watt[att_of(n) % 2][:, 1152:1280], start=True, stop=True)
                    ins.then_inc(written[RING[s] % BANKS], 1)
                elif s[0] == "route":
                    L, b = s[1], s[2]
                    wait_done(pe, ("turn", MOE + 2 * L + b))
                    for t in range(NT):
                        ins = pe.matmul(bank[:, t * E:(t + 1) * E], hT[b][:, t * 128:(t + 1) * 128],
                                        cols[:, COL_RW + L * E:COL_RW + (L + 1) * E], start=True, stop=True)
                    ins.then_inc(written[RING[s] % BANKS], 1)
                elif s[0] == "fc1":
                    L, k = s[1], s[2]
                    e, b = PAIRS[k]
                    i = (L * E + e) % WSLOT
                    pe.wait_ge(w_split, 2 * (L * E + e + 1))
                    if e == 0:
                        wait_done(pe, ("turn", MOE + 2 * L + b))
                        pe.wait_ge(hlo_ready, 2 * L + b + 1)
                    if k == 0:
                        pe.wait_ge(probs_ready, units_before(16 * (L + 1)))
                    for c in range(NC):
                        f = 64 * L + NC * k + c
                        if f >= 4:
                            pe.wait_ge(hidden_ready, f - 3)
                        m = slice(c * 128, (c + 1) * 128)
                        pe.matmul(fc1_bank(f), w_hi[i][:, m], hT_hi[b][:, :], start=True, stop=False)
                        pe.matmul(fc1_bank(f), w_hi[i][:, m], hT_lo[b][:, :], start=False, stop=False)
                        pe.matmul(fc1_bank(f), w_lo[i][:, m], hT_hi[b][:, :], start=False,
                                  stop=True).then_inc(fc1_written, 1)
                elif s[0] == "cbc":
                    L, k = s[1], s[2]
                    e, b = PAIRS[k]
                    if e == 0:
                        pe.wait_ge(comb_ready, 2 * L + b + 1)
                    if k == 0:
                        pe.wait_ge(o_ready, 16 * (L + 1))
                    if 16 * L + k:
                        pe.wait_ge(gate_ready, 16 * L + k)
                    for t in range(NT):
                        ins = pe.transpose(ps_o[:, t * 128:(t + 1) * 128],
                                           comb[b][:, t, e:e + 1].to_broadcast([128, 128]), ident[:, :])
                    ins.then_inc(gate_written, 1)
                elif s[0] == "fc2":
                    L, k = s[1], s[2]
                    i = (L * E + PAIRS[k][0]) % WSLOT
                    pe.wait_ge(w_loaded[i], 32 * ((L * E + PAIRS[k][0]) // WSLOT + 1))
                    for c in range(NC):
                        pe.wait_ge(hidden_ready, 64 * L + NC * k + c + 1)
                        ins = pe.matmul(bank[:, :], w2[i][:, c * 128:(c + 1) * 128], hidden(k, c),
                                        start=c == 0, stop=c == NC - 1)
                    ins.then_inc(written[RING[s] % BANKS], 1)
                elif s[0] == "mout":
                    L, b = s[1], s[2]
                    pe.wait_ge(acc_added, ADDS[L, PAIRS.index((E - 1, b))] + 1)
                    for t in range(NT):
                        ins = pe.transpose(bank[:, t * 128:(t + 1) * 128], acc[b][:, t * 128:(t + 1) * 128],
                                           ident[:, :])
                    ins.then_inc(written[RING[s] % BANKS], 1)

        @block.vector
        def _(dve):
            chain = [0]

            def link(ins):
                chain[0] += 1
                ins.then_inc(dve_chain, 1)
                dve.wait_ge(dve_chain, chain[0])

            def tiles(ap):
                return ap.rearrange("p (t d) -> p t d", d=128)

            for t in v_aug:
                dve.memset(t[:, :, :, :], 0.0)
            link(dve.memset(vc_aug[:, :, :, :], 0.0))
            for t in v_aug:
                dve.memset(t[:, :, :, HD:HD + 1], 1.0)
            link(dve.memset(vc_aug[:, :, :, HD:HD + 1], 1.0))
            dve.wait_ge(ident_ready, 1)
            dve.wait_ge(consts_loaded, 16)
            exps = 0
            masks_made = False
            for s in PLAN:
                if s[0] in ("vproj", "cvproj", "mt", "otr", "oproj", "route", "mout", "max", "fc2"):
                    wait_written(dve, s)
                    bank = bank_of(s)
                if s[0] == "norm":
                    d = s[1]
                    if d == "ctx":
                        i, p, src, dst = 2, SE, ctx_x, ctx_hat
                        dve.wait_ge(ctx_loaded, 16)
                    else:
                        i, p, src, dst = d % 2, 128, x[d % 2], xhat[d % 2]
                        if d < 2:
                            dve.wait_ge(x_loaded, 16 * B)
                    nt = src.shape[1]
                    for t in range(nt):
                        ins = dve.bn_stats(stats[0:p, i, t, :], src[:, t, :])
                    link(ins)
                    for t in range(nt):
                        ins = dve.bn_aggr(mv[0:p, i, t, :], stats[0:p, i, t, :])
                    link(ins)
                    v, y, sq = rstd[0:p, i, 0, 0:nt], rstd[0:p, i, 3, 0:nt], rstd[0:p, i, 2, 0:nt]
                    link(dve.tensor_scalar_add(v, mv[0:p, i, 0:nt, 1], EPS))
                    link(dve.tensor_single_scalar(sq.bitcast(i32), v.bitcast(i32), 1, ALU.logical_shift_right))
                    link(dve.tensor_scalar(y.bitcast(i32), sq.bitcast(i32), -1, HALF_MAGIC, ALU.mult, ALU.add))
                    for _ in range(NEWTON):
                        link(dve.scalar_tensor_tensor(sq, y, -0.5, y, ALU.mult, ALU.mult))
                        link(dve.tensor_tensor(sq, sq, v, ALU.mult))
                        link(dve.scalar_tensor_tensor(y, sq, 1.5, y, ALU.add, ALU.mult))
                    for t in range(nt):
                        ins = dve.tensor_scalar(dst[:, t, :], src[:, t, :], mv[0:p, i, t, 0:1],
                                                rstd[0:p, i, 3, t:t + 1], ALU.subtract, ALU.mult)
                    ins.then_inc(xhat_ready, 1)
                elif s[0] == "vproj":
                    n = s[1]
                    dve.wait_ge(rows_ready, 1)
                    if n >= 4:
                        dve.wait_ge(av_done, avs_before(4 * (n - 3)))
                    dve.tensor_tensor(
                        v_aug[n % 2][:, :, :, 0:HD], bank[:, :].rearrange("p (t h d) -> p t h d", t=NT, h=H),
                        row(ROW_BV + att_of(n)).rearrange("p t (h d) -> p t h d", h=H), ALU.add).then_inc(done[RING[s] % BANKS], 1)
                elif s[0] == "cvproj":
                    L = s[1]
                    dve.wait_ge(rows_ready, 1)
                    if L == 1:
                        dve.wait_ge(av_done, avs_before(16))
                    dve.tensor_tensor(
                        vc_aug[:, :, :, 0:HD],
                        bank[0:SE, 0:B * 128].rearrange("p (t h d) -> p t h d", t=B, h=H),
                        row(ROW_BV + 2 * L + 1, SE, B).rearrange("p t (h d) -> p t h d", h=H),
                        ALU.add).then_inc(done[RING[s] % BANKS], 1)
                elif s[0] == "max":
                    G, i = s[1], s[2]
                    n = G // NG
                    if is_self(n):
                        qb, j = divmod(i, GH)
                        w = (qb + 1) * 128 if causal(n) else S
                        dve.tensor_reduce(m_raw[G % 2][:, qb, j:j + 1], bank[:, 0:w], AX.X,
                                          ALU.max).then_inc(done[RING[s] % BANKS], 1)
                    else:
                        dve.tensor_reduce(m_raw[G % 2][:, i, :], tiles(bank[:, :])[:, :, 0:SE], AX.X,
                                          ALU.max).then_inc(done[RING[s] % BANKS], 1)
                elif s[0] == "mcols":
                    G = s[1]
                    dve.wait_ge(pads_ready, 1)
                    wait_done(dve, ("max", G, n_max(G // NG) - 1))
                    heads = m_cols[:, :, :].rearrange("p t (j c) -> p t j c", c=32)
                    hi, lo = heads[:, :, :, 24], heads[:, :, :, 25]
                    link(dve.tensor_scalar(hi.bitcast(f32r), m_raw[G % 2][:, :, :], -1.0, None, ALU.mult))
                    dve.scalar_tensor_tensor(lo, m_raw[G % 2][:, :, :], -1.0, hi, ALU.mult,
                                             ALU.subtract).then_inc(mcols_ready, 1)
                elif s[0] == "mt":
                    G = s[1]
                    dve.wait_ge(stack_ready, SPLIT[("proj", G, "q")] + 1)
                    if G >= 2:
                        dve.wait_ge(scores_written, units_before(G - 1))
                    dve.tensor_tensor(q_max[G % 2][:, :], bank[:, :], q_st[G % QRING][:, :].bitcast(f32),
                                      ALU.add).then_inc(done[RING[s] % BANKS], 1)
                    if not masks_made:
                        masks_made = True
                        dve.wait_ge(masks_ready, 1)
                        dve.tensor_copy(ident_r[:, :], ident[:, :])
                        dve.tensor_copy(mask_r[:, :, :], mask[:, :, :]).then_inc(masks_ready, 1)
                elif s[0] == "otr":
                    G = s[1]
                    b, g = G // NG % 2, G % NG
                    o = bank[:, :].rearrange("p (i c) -> p i c", c=32)
                    if G >= 2:
                        wait_done(dve, ("otr", G - 2))
                    link(dve.reciprocal(rden[G % 2][:, :], o[:, :, HD]))
                    dve.tensor_tensor(a_tok[b][:, :, g * 32:(g + 1) * 32].rearrange("p t (j d) -> p t j d", d=HD),
                                      bank[:, :].rearrange("p (t j c) -> p t j c", j=GH, c=32)[:, :, :, 0:HD],
                                      rden[G % 2][:, :].rearrange("p (t j) -> p t j", j=GH).unsqueeze(3)
                                      .to_broadcast([128, NT, GH, HD]), ALU.mult).then_inc(done[RING[s] % BANKS], 1)
                elif s[0] == "oproj":
                    n = s[1]
                    b = n % 2
                    dve.wait_ge(res_ready, ORD[("resid", n)] + 1)
                    dve.tensor_tensor(x[b][:, :, :], tiles(bank[:, :]), res[b][:, :, :],
                                      ALU.add).then_inc(done[RING[s] % BANKS], 1)
                    wait_done(dve, s)
                elif s[0] == "route":
                    L, b = s[1], s[2]

                    def top(lg, m, one):
                        link(dve.tensor_reduce(rs[:, m, :], lg, AX.X, ALU.max))
                        link(dve.tensor_tensor(r[:, 3, :, :], lg, over_experts(rs[:, m, :]), ALU.is_equal))
                        link(dve.tensor_tensor(r[:, 3, :, :], r[:, 3, :, :],
                                               over_tiles(cols[:, COL_DESC:COL_DESC + E]), ALU.mult))
                        link(dve.tensor_reduce(rs[:, 0, :], r[:, 3, :, :], AX.X, ALU.max))
                        link(dve.tensor_tensor(one, r[:, 3, :, :], over_experts(rs[:, 0, :]), ALU.is_equal))

                    lg, one1, one2, rest = r[:, 0, :, :], r[:, 4, :, :], r[:, 5, :, :], r[:, 6, :, :]
                    dve.tensor_tensor(lg, bank[:, 0:NT * E].rearrange("p (t e) -> p t e", e=E),
                                      over_tiles(cols[:, COL_RB + L * E:COL_RB + (L + 1) * E]),
                                      ALU.add).then_inc(done[RING[s] % BANKS], 1)
                    wait_done(dve, s)
                    if L == 1:
                        link(dve.tensor_reduce(rs[:, 0, :], lg, AX.X, ALU.max))
                        dve.tensor_tensor(r[:, 1, :, :], lg, over_experts(rs[:, 0, :]),
                                          ALU.subtract).then_inc(exp_in, 1)
                        exps += 1
                        dve.wait_ge(exp_out, exps)
                        link(dve.tensor_reduce(rs[:, 1, :], r[:, 2, :, :], AX.X, ALU.add))
                        link(dve.reciprocal(rs[:, 2, :], rs[:, 1, :]))
                        link(dve.tensor_tensor(lg, r[:, 2, :, :], over_experts(rs[:, 2, :]), ALU.mult))
                    top(lg, 3, one1)
                    link(dve.scalar_tensor_tensor(rest, one1, -BIG, lg, ALU.mult, ALU.add))
                    top(rest, 4, one2)
                    dve.tensor_tensor(rs[:, 7, :], rs[:, 4, :], rs[:, 3, :], ALU.subtract).then_inc(exp_in, 1)
                    exps += 1
                    dve.wait_ge(exp_out, exps)
                    link(dve.tensor_scalar_add(rs[:, 5, :], rs[:, 8, :], 1.0))
                    link(dve.reciprocal(rs[:, 6, :], rs[:, 5, :]))
                    dve.tensor_tensor(one1, one1, over_experts(rs[:, 6, :]), ALU.mult)
                    link(dve.tensor_tensor(rs[:, 5, :], rs[:, 8, :], rs[:, 6, :], ALU.mult))
                    link(dve.tensor_tensor(one2, one2, over_experts(rs[:, 5, :]), ALU.mult))
                    dve.tensor_tensor(comb[b][:, :, :], one1, one2, ALU.add).then_inc(comb_ready, 1)
                elif s[0] == "fc2":
                    L, k = s[1], s[2]
                    e, b = PAIRS[k]
                    dve.wait_ge(gate_ready, 16 * L + k + 1)
                    if ADDS[L, k]:
                        dve.wait_ge(acc_added, ADDS[L, max(k - 1, 0)])
                    dst = acc[b] if e == 0 else eo[k % 2]
                    dve.scalar_tensor_tensor(dst[:, :], bank[:, :], col(COL_B2 + L * E + e),
                                             gate_bc[k % 2][:, :], ALU.add, ALU.mult).then_inc(done[RING[s] % BANKS], 1)
                elif s[0] == "mout":
                    L, b = s[1], s[2]
                    if L == 1:
                        dve.wait_ge(res_ready, ORD[("resid", MOE + 2 + b)] + 1)
                    dve.tensor_tensor(x[b][:, :, :], tiles(bank[:, :]), (x if L == 0 else res)[b][:, :, :],
                                      ALU.add).then_inc(done[RING[s] % BANKS], 1)
                    wait_done(dve, s)
                elif s[0] == "final":
                    b = s[1]
                    dve.wait_ge(xhat_ready, ORD[("norm", LAST + b)] + 1)
                    link(dve.tensor_tensor(xhat[b][:, :, :], xhat[b][:, :, :], row(ROW_LN + 4), ALU.mult))
                    dve.tensor_tensor(res[b][:, :, :], xhat[b][:, :, :], row(ROW_LN + 5), ALU.add).then_inc(final_ready, 1)


ATTENTIONS = ("L0_xattn_sa", "L0_xattn_ca", "L1_xattn_sa", "L1_xattn_ca")


def attention_weights(inputs, np, a):
    t = ATTENTIONS[a]
    if a < 2:
        w, b = inputs[t + "_in_w"], inputs[t + "_in_b"]
        ws = [w[i * D:(i + 1) * D].T for i in range(3)] + [inputs[t + "_out_w"].T]
        bs = [b[i * D:(i + 1) * D] for i in range(3)] + [inputs[t + "_out_b"]]
    else:
        ws = [inputs[t + "_w" + c] for c in "qkvo"]
        bs = [inputs[t + "_b" + c] for c in "qkvo"]
    return ws, bs


def stack_heads(w, np):
    w = w.reshape(-1, NG, GH, 1, HD)
    return np.concatenate([w, w, w, np.zeros_like(w)], axis=3).reshape(-1, NG, GH * 32)


def kernel(**inputs):
    import numpy as np
    import concourse.bacc as bacc
    from concourse.bass_utils import run_bass_kernel_spmd

    inputs = {k: np.asarray(v) for k, v in inputs.items()}
    f = np.float32
    cols = np.zeros((128, NCOL), f)
    rows = np.zeros((NROW, 128), f)
    watt = np.zeros((4, 128, ATT), f)
    row_of = np.arange(128) % 32
    for a in range(4):
        (wq, wk, wv, wo), (bq, bk, bv, bo) = attention_weights(inputs, np, a)
        watt[a, :, 0:512] = stack_heads(wq, np).reshape(128, 512)
        watt[a, :, 512:1024] = stack_heads(wk, np).reshape(128, 512)
        watt[a, :, 1024:1152], watt[a, :, 1152:1280] = wv, wo
        cols[:, COL_BQ + 4 * a:COL_BQ + 4 * a + 4] = stack_heads(bq[None], np)[0].T
        cols[:, COL_BK + 4 * a:COL_BK + 4 * a + 4] = stack_heads(bk[None], np)[0].T
        rows[ROW_BV + a], rows[ROW_BO + a] = bv, bo
    cols[(row_of == 24) | (row_of == 25), COL_BK:COL_BK + 16] = 1.0
    norms = ("L0_xattn_sa_ln", "L0_xattn_ca_q_ln", "L0_xattn_ca_kv_ln", "L0_xattn_moe_ln", "L1_xattn_ln1", "L1_xattn_ln2")
    for i, t in enumerate(norms):
        cols[:, COL_LN + 2 * i], cols[:, COL_LN + 2 * i + 1] = inputs[t + "_g"], inputs[t + "_b"]
    for i in range(3):
        rows[ROW_LN + 2 * i], rows[ROW_LN + 2 * i + 1] = inputs[f"L1_xattn_ln{i + 1}_g"], inputs[f"L1_xattn_ln{i + 1}_b"]
    q_lo, k_lo = row_of // HD == 2, row_of // HD == 1
    cols[q_lo, COL_QLO], cols[k_lo, COL_KLO] = 1.0, 1.0
    cols[q_lo, COL_BQL:COL_BQL + 16] = cols[q_lo, COL_BQ:COL_BQ + 16]
    cols[k_lo, COL_BKL:COL_BKL + 16] = cols[k_lo, COL_BK:COL_BK + 16]
    cols[:, COL_EPS], cols[:, COL_ONE] = EPS, 1.0
    cols[:, COL_DESC:COL_DESC + E] = np.arange(E, 0, -1)
    w = np.zeros((2 * E, 128, 2 * F), f)
    experts = ((inputs["L0_xattn_e_fc1_w"].transpose(0, 2, 1), inputs["L0_xattn_e_fc2_w"].transpose(0, 2, 1),
                inputs["L0_xattn_e_fc1_b"], inputs["L0_xattn_e_fc2_b"], inputs["L0_xattn_router_w"].T,
                inputs["L0_xattn_router_b"]),
               (inputs["L1_xattn_e_w1"], inputs["L1_xattn_e_w2"], inputs["L1_xattn_e_b1"], inputs["L1_xattn_e_b2"],
                inputs["L1_xattn_router_w"], inputs["L1_xattn_router_b"]))
    for L, (w1, w2, b1, b2, rw, rb) in enumerate(experts):
        w[L * E:(L + 1) * E, :, 0:F] = w1
        w[L * E:(L + 1) * E, :, F:2 * F] = w2.reshape(E, NC, 128, D).transpose(0, 2, 1, 3).reshape(E, 128, F)
        cols[:, COL_B1 + L * E * NC:COL_B1 + (L + 1) * E * NC] = b1.reshape(E * NC, 128).T
        cols[:, COL_B2 + L * E:COL_B2 + (L + 1) * E] = b2.T
        cols[:, COL_RW + L * E:COL_RW + (L + 1) * E] = rw
        cols[:, COL_RB + L * E:COL_RB + (L + 1) * E] = rb[None]
    arrays = {
        "in_x": np.ascontiguousarray(inputs["x"].reshape(B, NT, 128, D).transpose(2, 0, 1, 3)),
        "in_ctx": np.ascontiguousarray(inputs["ctx_1024"].transpose(1, 0, 2)),
        "in_watt": watt, "in_cols": cols, "in_rows": rows, "in_w": w,
    }
    nc = bacc.Bacc("TRN2", target_bir_lowering=False, num_devices=1)
    args = [nc.dram_tensor(name, a.shape, mybir.dt.float32, kind="ExternalInput").ap() for name, a in arrays.items()]
    args.append(nc.dram_tensor("out_0", (128, B, NT, D), mybir.dt.float32, kind="ExternalOutput").ap())
    build(nc, *args)
    got = run_bass_kernel_spmd(nc, [arrays], core_ids=[0]).results[0]["out_0"]
    return np.ascontiguousarray(np.asarray(got).transpose(1, 2, 0, 3)).reshape(B, S, D)
```
